# Optimizing a Trainium2 kernel written in Bass

```python
import numpy as np
import jax
import jax.numpy as jnp

def _softmax(x, axis=-1):
    return jax.nn.softmax(x, axis=axis)

def _gelu(x):
    return jax.nn.gelu(x, approximate=True)

def _silu(x):
    return jax.nn.silu(x)

def _sigmoid(x):
    return jax.nn.sigmoid(x)

def _layernorm(x, axis=-1, eps=1e-05):
    m = jnp.mean(x, axis=axis, keepdims=True)
    v = jnp.var(x, axis=axis, keepdims=True)
    return (x - m) / jnp.sqrt(v + eps)

def _scatter_add(tgt, idx, src, axis=0):
    return tgt.at[idx].add(src)

def _segment_sum(src, seg, n):
    return jax.ops.segment_sum(src, seg, n)
kernel_name = 'mk_adaln_d1_jaxref_r8_f73b33'

def setup_inputs(seed: int=0):
    np.random.seed(seed)
    _w = jnp.asarray

    def _L0_attn_setup():
        import jax, jax.numpy as jnp
        import numpy as np
        HEADS = 16
        DIM_HEAD = 128
        SCALE = 16.0
        EPS = 1e-05

        def _layernorm(x, g):
            mu = jnp.mean(x, axis=-1, keepdims=True)
            var = jnp.mean((x - mu) ** 2, axis=-1, keepdims=True)
            return (x - mu) * jax.lax.rsqrt(var + EPS) * g

        def _l2norm(t):
            return t * jax.lax.rsqrt(jnp.sum(t * t, axis=-1, keepdims=True) + 1e-12)
        key = jax.random.key(seed)
        ks = jax.random.split(key, 5)
        B, N, dim = (2, 256, 256)
        hidden = HEADS * DIM_HEAD
        x = jax.random.normal(ks[0], (B, N, dim), dtype=jnp.float32)
        g_norm = jnp.ones((dim,), dtype=jnp.float32)
        Wq = jax.random.normal(ks[1], (dim, hidden), dtype=jnp.float32) * dim ** (-0.5)
        Wkv = jax.random.normal(ks[2], (dim, 2 * DIM_HEAD), dtype=jnp.float32) * dim ** (-0.5)
        Wout = jax.random.normal(ks[3], (hidden, dim), dtype=jnp.float32) * hidden ** (-0.5)
        g_out = jnp.ones((dim,), dtype=jnp.float32)
        return {'x': x, 'g_norm': g_norm, 'Wq': Wq, 'Wkv': Wkv, 'Wout': Wout, 'g_out': g_out}
    _L0_attn_in = _L0_attn_setup()

    def _L0_ffn_setup():
        import jax, jax.numpy as jnp
        import numpy as np
        DIM = 256
        N_EXPERTS = 8
        TOP_K = 2
        key = jax.random.key(seed)
        ks = jax.random.split(key, 5)
        x = jax.random.normal(ks[0], (4, 512, DIM), dtype=jnp.float32)
        W_up = jax.random.normal(ks[1], (DIM, DIM), dtype=jnp.float32) * (1.0 / np.sqrt(DIM))
        W_down = jax.random.normal(ks[2], (DIM, DIM), dtype=jnp.float32) * (1.0 / np.sqrt(DIM))
        W_gate = jax.random.normal(ks[3], (N_EXPERTS, DIM), dtype=jnp.float32) * (1.0 / np.sqrt(DIM))
        W_expert = jax.random.normal(ks[4], (DIM, DIM), dtype=jnp.float32) * (1.0 / np.sqrt(DIM))
        return {'x': x, 'W_up': W_up, 'W_down': W_down, 'W_gate': W_gate, 'W_expert': W_expert}
    _L0_ffn_in = _L0_ffn_setup()
    _L0_c = _w((lambda *s: np.random.randn(*s).astype(np.float32) * 0.05)(16, 256))
    _L0_wmod = _w((lambda *s: np.random.randn(*s).astype(np.float32) * 0.05)(256, 6 * 256) * 256 ** (-0.5))
    _d = {'L0_attn_x': _L0_attn_in['x'], 'L0_attn_g_norm': _L0_attn_in['g_norm'], 'L0_attn_Wq': _L0_attn_in['Wq'], 'L0_attn_Wkv': _L0_attn_in['Wkv'], 'L0_attn_Wout': _L0_attn_in['Wout'], 'L0_attn_g_out': _L0_attn_in['g_out'], 'L0_ffn_W_up': _L0_ffn_in['W_up'], 'L0_ffn_W_down': _L0_ffn_in['W_down'], 'L0_ffn_W_gate': _L0_ffn_in['W_gate'], 'L0_ffn_W_expert': _L0_ffn_in['W_expert'], 'L0_c': _L0_c, 'L0_wmod': _L0_wmod}
    _x0 = _d['L0_attn_x']
    _d['L0_attn_x'] = jax.random.normal(jax.random.fold_in(jax.random.key(seed), 1), (16, 256, 256), dtype=_x0.dtype)
    del _x0
    return _d

def reference(L0_attn_x, L0_attn_g_norm, L0_attn_Wq, L0_attn_Wkv, L0_attn_Wout, L0_attn_g_out, L0_ffn_W_up, L0_ffn_W_down, L0_ffn_W_gate, L0_ffn_W_expert, L0_c, L0_wmod):

    def _L0_attn_ref(x, g_norm, Wq, Wkv, Wout, g_out):
        import jax, jax.numpy as jnp
        import numpy as np
        HEADS = 16
        DIM_HEAD = 128
        SCALE = 16.0
        EPS = 1e-05

        def _layernorm(x, g):
            mu = jnp.mean(x, axis=-1, keepdims=True)
            var = jnp.mean((x - mu) ** 2, axis=-1, keepdims=True)
            return (x - mu) * jax.lax.rsqrt(var + EPS) * g

        def _l2norm(t):
            return t * jax.lax.rsqrt(jnp.sum(t * t, axis=-1, keepdims=True) + 1e-12)
        B, N, dim = x.shape
        xn = _layernorm(x, g_norm)
        q = xn @ Wq
        kv = xn @ Wkv
        k, v = (kv[..., :DIM_HEAD], kv[..., DIM_HEAD:])
        q = q.reshape(B, N, HEADS, DIM_HEAD).transpose(0, 2, 1, 3)
        q = q * SCALE
        q = _l2norm(q)
        k = _l2norm(k)
        s = jnp.sqrt(SCALE).astype(x.dtype)
        q = q * s
        k = k * s
        sim = jnp.einsum('bhid,bjd->bhij', q, k)
        attn = jax.nn.softmax(sim.astype(jnp.float32), axis=-1).astype(sim.dtype)
        out = jnp.einsum('bhij,bjd->bhid', attn, v)
        out = out.transpose(0, 2, 1, 3).reshape(B, N, HEADS * DIM_HEAD)
        out = out @ Wout
        return _layernorm(out, g_out)

    def _L0_ffn_ref(x, W_up, W_down, W_gate, W_expert):
        import jax, jax.numpy as jnp
        import numpy as np
        DIM = 256
        N_EXPERTS = 8
        TOP_K = 2
        logits = jnp.einsum('bsd,ed->bse', x, W_gate)
        routing_weights, selected_experts = jax.lax.top_k(logits, TOP_K)
        shared_out = jnp.einsum('bsd,od->bso', jax.nn.relu(jnp.einsum('bsd,od->bso', x, W_up)), W_down)
        rw = jax.nn.softmax(routing_weights, axis=-1)
        expert_out = jnp.einsum('bsd,do->bso', x, W_expert)
        moe_out = jnp.sum(rw, axis=-1, keepdims=True) * expert_out
        return shared_out + moe_out
    x = L0_attn_x
    mod = (_silu(L0_c) @ L0_wmod).reshape(L0_c.shape[0], 6, 1, -1)
    sa, ca, ga, sb, cb, gb = (mod[:, 0], mod[:, 1], mod[:, 2], mod[:, 3], mod[:, 4], mod[:, 5])
    ga = (2 * (ga >= 0) - 1) * jnp.maximum(jnp.abs(ga), 0.25)
    gb = (2 * (gb >= 0) - 1) * jnp.maximum(jnp.abs(gb), 0.25)
    h = _layernorm(x, axis=-1) * (1 + ca) + sa
    x = x + ga * _L0_attn_ref(h, L0_attn_g_norm, L0_attn_Wq, L0_attn_Wkv, L0_attn_Wout, L0_attn_g_out)
    h = _layernorm(x, axis=-1) * (1 + cb) + sb
    x = x + gb * _L0_ffn_ref(h, L0_ffn_W_up, L0_ffn_W_down, L0_ffn_W_gate, L0_ffn_W_expert)
    return x

_drawn_inputs = setup_inputs


def setup_inputs(seed=0):
    import zlib

    import numpy as np

    out = dict(_drawn_inputs(seed))
    spreads = {'L0_attn_g_norm': (1.0, 0.2), 'L0_attn_g_out': (1.0, 0.2)}
    factors = {}
    for name, (base, spread) in spreads.items():
        noise = np.random.default_rng([zlib.crc32(name.encode()), seed]).standard_normal(out[name].shape)
        drawn = base * np.exp(spread * noise) if base else spread * noise
        out[name] = jnp.asarray(drawn.astype(out[name].dtype))
    for name, factor in factors.items():
        out[name] = (out[name] * factor).astype(out[name].dtype)
    return out
```

```python
from contextlib import ExitStack

import concourse.bass as bass
from concourse import mybir

F32 = mybir.dt.float32
F32R = mybir.dt.float32r
ALU = mybir.AluOpType
ACT = mybir.ActivationFunctionType


B, N, D = 16, 256, 256
HEADS, DH = 16, 128
P = 128
DC = D // P
PAIRS = B // 2
TOK = 2 * N
KT = N // P
TILES = TOK // P
EXPERTS = 8
EG = D + EXPERTS
LN_EPS = 1e-5
SCALE = 16.0
L2_EPS = 1e-12
ONE = 1.0 / SCALE
LN_OPS = 3 * TILES + 4
E_MOD = 12
MOD_FIX = 13
GATE = 4 + 5


def adaln_block(nc, x, g_norm_pc, wq, wkv, wo, g_out, wup_t, wdown_t, wgate_t, wexp, c_t, wmod, scratch, out):
    x_v = x.rearrange("(u b) (j p) d -> u p b j d", b=2, p=P)
    out_v = out.rearrange("(u b) (j p) d -> u p b j d", b=2, p=P)
    mod_v = scratch.rearrange("(u b) k d -> u b k d", b=2)

    with ExitStack() as ctx:
        def sb(name, shape, dt=F32):
            return ctx.enter_context(nc.sbuf_tensor(name, shape, dt))

        def psum(name, shape):
            return ctx.enter_context(nc.psum_tensor(name, shape, F32))

        def sem(name):
            return ctx.enter_context(nc.semaphore(name))

        ps_q = psum("ps_q", [P, TOK])
        ps_s = psum("ps_s", [P, TOK])
        ps_sim = psum("ps_sim", [P, KT, TOK])
        ps_o = psum("ps_o", [P, TOK])
        ps_out = psum("ps_out", [P, TILES, D])
        ps_x = psum("ps_x", [P, TOK])

        wq_h, wq_l = sb("wq_h", [P, DC, HEADS * DH], F32R), sb("wq_l", [P, DC, HEADS * DH], F32R)
        wo_h, wo_l = sb("wo_h", [P, HEADS, D], F32R), sb("wo_l", [P, HEADS, D], F32R)
        wkv_h, wkv_l = sb("wkv_h", [P, DC, 2 * DH], F32R), sb("wkv_l", [P, DC, 2 * DH], F32R)
        wup_h, wup_l = sb("wup_h", [P, DC, D], F32R), sb("wup_l", [P, DC, D], F32R)
        wdn_h, wdn_l = sb("wdn_h", [P, DC, D], F32R), sb("wdn_l", [P, DC, D], F32R)
        weg_h, weg_l = sb("weg_h", [P, DC, EG], F32R), sb("weg_l", [P, DC, EG], F32R)
        ones = sb("ones", [P, P], F32R)
        ident = sb("ident", [P, P])
        gn = sb("gn", [P, DC])

        xn_h, xn_l = sb("xn_h", [P, DC, TOK], F32R), sb("xn_l", [P, DC, TOK], F32R)
        xc_h, xc_l = sb("xc_h", [P, DC, TOK], F32R), sb("xc_l", [P, DC, TOK], F32R)
        k_h, k_l = sb("k_h", [P, TOK], F32R), sb("k_l", [P, TOK], F32R)
        v_h, v_l = sb("v_h", [P, TILES, DH], F32R), sb("v_l", [P, TILES, DH], F32R)
        xin = sb("xin", [P, 2, KT, D])
        xin_flat = xin[:, :, :, :].rearrange("p b j d -> p (b j d)")
        ksq, kn = xin_flat[:, 0:TOK], xin_flat[:, TOK:2 * TOK]
        kr, vt = ksq, ksq
        ksq_h, ksq_l = sb("ksq_h", [P, TOK], F32R), sb("ksq_l", [P, TOK], F32R)
        mod_a = sb("mod_a", [P, 2, 2, D])
        late = sb("late", [P, 2, 2048])
        mod_b = late[:, 0, :].rearrange("p (b k d) -> p b k d", b=2, k=4)
        xres = late[:, 1, 0:1024].rearrange("p (b j d) -> p b j d", b=2, j=KT)
        ox = late[:, 1, 1024:2048].rearrange("p (b j d) -> p b j d", b=2, j=KT)
        ht_h, ht_l = sb("ht_h", [P, DC, TOK], F32R), sb("ht_l", [P, DC, TOK], F32R)
        rt_h, rt_l = sb("rt_h", [P, DC, TOK], F32R), sb("rt_l", [P, DC, TOK], F32R)
        ex = sb("ex", [P, TILES, EG])

        sq = sb("sq", [P, TOK])
        sq_h, sq_l = sb("sq_h", [P, TOK], F32R), sb("sq_l", [P, TOK], F32R)
        fones = sq[:, TOK - P:TOK]
        q_work = sb("q_work", [P, 2, TOK])
        rq, qn = q_work[:, 0, :], q_work[:, 1, :]
        q_h, q_l = sb("q_h", [P, TOK], F32R), sb("q_l", [P, TOK], F32R)
        pr = sb("pr", [P, KT, TOK])
        pr_h, pr_l = sb("pr_h", [P, 2, KT, TOK], F32R), sb("pr_l", [P, 2, KT, TOK], F32R)
        ss = sb("ss", [P, TOK])
        ss_h, ss_l = sb("ss_h", [P, TOK], F32R), sb("ss_l", [P, TOK], F32R)
        o_work = sb("o_work", [P, 2, TOK])
        rden, on = o_work[:, 0, :], o_work[:, 1, :]
        o_h, o_l = sb("o_h", [P, TOK], F32R), sb("o_l", [P, TOK], F32R)

        ln_p = (sb("st_p", [P, TILES, 6]), sb("mv_p", [P, TILES, 2]), sb("y0_p", [P, TILES]), sb("nf_p", [P, TILES]), sb("rs_p", [P, TILES]))
        ln_e = (sb("st_e", [P, TILES, 6]), sb("mv_e", [P, TILES, 2]), sb("y0_e", [P, TILES]), sb("nf_e", [P, TILES]), sb("rs_e", [P, TILES]))
        eps_ln, eps_q, eps_k = sb("eps_ln", [P, 1]), sb("eps_q", [P, 1]), sb("eps_k", [P, 1])
        top = sb("top", [P, TILES, 8])
        g_d, g_e, g_r = sb("g_d", [P, TILES, 2]), sb("g_e", [P, TILES, 2]), sb("g_r", [P, TILES, 2])
        g_s, g_i, g_w = sb("g_s", [P, TILES]), sb("g_i", [P, TILES]), sb("g_w", [P, TILES])
        c_sb, c_e, c_s = sb("c_sb", [P, DC, B]), sb("c_e", [P, DC, B]), sb("c_s", [P, DC, B])
        gout16 = sq[0:B, 0:D]
        mod_rows = (pr[0:B, :, :].rearrange("b c (k d) -> b (c k) d", d=D),
                    q_work[0:B, 0, :].rearrange("b (k d) -> b k d", d=D))

        c_in, gn_in, gout_in = sem("c_in"), sem("gn_in"), sem("gout_in")
        wmod_in = [sem(f"wmod_in{n}") for n in range(3)]
        wkv_in, w2_in = sem("wkv_in"), sem("w2_in")
        stage_in = [sem("stage_in0"), sem("stage_in1")]
        xin_in, moda_in, xres_in, modb_in = sem("xin_in"), sem("moda_in"), sem("xres_in"), sem("modb_in")
        out_stored, mod_stored = sem("out_stored"), sem("mod_stored")
        const_zero, const_done, ones_done, eps_done = sem("const_zero"), sem("const_done"), sem("ones_done"), sem("eps_done")
        w_hi, w_lo = sem("w_hi"), sem("w_lo")
        wkv_hi, wkv_lo = sem("wkv_hi"), sem("wkv_lo")
        w2_hi, w2_lo = sem("w2_hi"), sem("w2_lo")
        c_exp, c_chain, mod_mm, mod_fix = sem("c_exp"), sem("c_chain"), sem("mod_mm"), sem("mod_fix")
        p_ln, p_mod, p_rs = sem("p_ln"), sem("p_mod"), sem("p_rs")
        xt_tr, xnh_done, xnl_done = sem("xt_tr"), sem("xnh_done"), sem("xnl_done")
        xch_done, xcl_done = sem("xch_done"), sem("xcl_done")
        kproj_done, ksq_done, ksqh_done, ksql_done = sem("kproj_done"), sem("ksq_done"), sem("ksqh_done"), sem("ksql_done")
        ksum_done, kln_done, rk_done, kn_done, kh_done, kl_done = sem("ksum_done"), sem("kln_done"), sem("rk_done"), sem("kn_done"), sem("kh_done"), sem("kl_done")
        vproj_done, vt_done, vtr_done, vh_done, vl_done = sem("vproj_done"), sem("vt_done"), sem("vtr_done"), sem("vh_done"), sem("vl_done")
        qproj_done, sq_done, sqh_done, sql_done = sem("qproj_done"), sem("sq_done"), sem("sqh_done"), sem("sql_done")
        qsum_done, qln_done, rq_done, qn_done, qh_done, ql_done = sem("qsum_done"), sem("qln_done"), sem("rq_done"), sem("qn_done"), sem("qh_done"), sem("ql_done")
        sim_done, exp_done, ph_done, pl_done = sem("sim_done"), sem("exp_done"), sem("ph_done"), sem("pl_done")
        ss_done, ssh_done, ssl_done, den_done = sem("ss_done"), sem("ssh_done"), sem("ssl_done"), sem("den_done")
        av_done, dln_done, rden_done, on_done, oh_done, ol_done = sem("av_done"), sem("dln_done"), sem("rden_done"), sem("on_done"), sem("oh_done"), sem("ol_done")
        out_done = sem("out_done")
        oxa_done, oxd_done, e_ln, e_mod, e_rs = sem("oxa_done"), sem("oxd_done"), sem("e_ln"), sem("e_mod"), sem("e_rs")
        h_tr, hh_done, hl_done = sem("h_tr"), sem("hh_done"), sem("hl_done")
        up_done, rh_done, rl_done = sem("up_done"), sem("rh_done"), sem("rl_done")
        xg_done, ex_done, gate, gate_exp = sem("xg_done"), sem("ex_done"), sem("gate"), sem("gate_exp")
        shared_done, f_done = sem("shared_done"), sem("f_done")

        def after(eng, s, value):
            if isinstance(value, int) and value <= 0:
                return
            eng.wait_ge(s, value)

        class Step:

            def __init__(self, t, t16, h, first, last, past=False):
                self.t, self.t16, self.h, self.first, self.last, self.past = t, t16, h, first, last, past

            def n(self, d, per=1, k=None):
                k = per if k is None else k
                base = self.t16 if per == 1 else self.t * (HEADS * per)
                return base + (per * (self.h + d) + k)

            def has(self, d):
                if self.past:
                    return d < 0
                return not (self.first and self.h + d < 0) and not (self.last and self.h + d >= HEADS)

        def run(eng, step):
            for h in range(HEADS):
                step(Step(0, 0, h, True, False))
            with eng.Fori(1, PAIRS - 1) as t:
                t16 = t * HEADS
                for h in range(HEADS):
                    step(Step(t, t16, h, False, False))
            for h in range(HEADS):
                step(Step(PAIRS - 1, (PAIRS - 1) * HEADS, h, False, True))

        END = [Step(PAIRS, PAIRS * HEADS, h, False, True, past=True) for h in range(2)]
        START = [Step(0, 0, h, False, False) for h in (-2, -1)]

        block = ctx.enter_context(nc.Block())

        @block.sync
        def _(sp):
            def load_x(u):
                sp.wait_ge(kl_done, u)
                sp.wait_ge(vtr_done, u)
                sp.dma_start(xin[:, :, :, :], x_v[u]).then_inc(xin_in, 16)
                sp.dma_start(mod_a[:, :, :, :], mod_v[u, :, 0:2, :].partition_broadcast(P)).then_inc(moda_in, 16)

            def load_late(w):
                after(sp, e_mod, w * E_MOD)
                sp.dma_start(mod_b, mod_v[w, :, 2:6, :].partition_broadcast(P)).then_inc(modb_in, 16)
                sp.dma_start(xres, x_v[w]).then_inc(xres_in, 16)

            def store(w):
                sp.wait_ge(e_mod, w * E_MOD + E_MOD)
                sp.dma_start(out_v[w], ox).then_inc(out_stored, 16)

            sp.dma_start(c_sb[:, :, :], c_t.rearrange("(c p) b -> p c b", p=P)).then_inc(c_in, 16)
            sp.dma_start(xin[:, :, :, :], x_v[0]).then_inc(xin_in, 16)
            wmod_v = wmod.rearrange("(c p) n -> p c n", p=P)
            for n, place in enumerate((pr, q_work, o_work)):
                sp.dma_start(place[:, :, :], wmod_v[:, :, n * 512:(n + 1) * 512]).then_inc(wmod_in[n], 16)
            sp.dma_start(gout16, g_out.partition_broadcast(B)).then_inc(gout_in, 16)
            sp.dma_start(gn[:, :], g_norm_pc).then_inc(gn_in, 16)
            sp.dma_start(ss[:, :].rearrange("p (c n) -> p c n", c=DC),
                         wkv.rearrange("(c p) n -> p c n", p=P)).then_inc(wkv_in, 16)
            wq_v = wq.rearrange("(c p) n -> c p n", p=P)
            wo_v = wo.rearrange("(g h p) n -> g p h n", g=2, p=P)
            for i in range(2):
                sp.dma_start(late[:, i, :], wq_v[i]).then_inc(stage_in[i], 16)
            sp.wait_ge(mod_stored, 32)
            sp.dma_start(mod_a[:, :, :, :], mod_v[0, :, 0:2, :].partition_broadcast(P)).then_inc(moda_in, 16)
            for i in range(2):
                sp.wait_ge(w_lo, i + 1)
                sp.dma_start(late[:, i, :].rearrange("p (h n) -> p h n", n=D), wo_v[i]).then_inc(stage_in[i], 16)
            stage2 = ex[:, :, :].rearrange("p j n -> p (j n)")
            for i, w in enumerate((None, wup_t, wdown_t)):
                after(sp, w2_lo, i)
                if w is None:
                    place = stage2[:, 0:DC * EG].rearrange("p (c n) -> p c n", c=DC)
                    sp.dma_start(place[:, :, 0:D], wexp.rearrange("(c p) n -> p c n", p=P)).then_inc(w2_in, 16)
                    sp.dma_start(place[:, :, D:EG], wgate_t.rearrange("(c p) n -> p c n", p=P)).then_inc(w2_in, 16)
                else:
                    sp.dma_start(stage2[:, 0:DC * D].rearrange("p (c n) -> p c n", c=DC),
                                 w.rearrange("(c p) n -> p c n", p=P)).then_inc(w2_in, 16)
            load_x(1)
            sp.wait_ge(w_lo, 4)
            with sp.Fori(1, PAIRS - 1) as t:
                load_late(t - 1)
                load_x(t + 1)
                store(t - 1)
            load_late(PAIRS - 2)
            store(PAIRS - 2)
            load_late(PAIRS - 1)
            store(PAIRS - 1)
            sp.wait_ge(out_stored, 16 * PAIRS)

        @block.tensor
        def _(pe):
            def mm3(o, wh, wl, mh, ml, start, stop, **kw):
                pe.matmul(o, wh, mh, start=start, stop=False, **kw)
                pe.matmul(o, wh, ml, start=False, stop=False, **kw)
                return pe.matmul(o, wl, mh, start=False, stop=stop, **kw)

            def project(o, wh, wl, cols, xh, xl):
                for c in range(DC):
                    last = mm3(o, wh[:, c, cols], wl[:, c, cols], xh[:, c, :], xl[:, c, :], c == 0, c == DC - 1)
                return last

            def column_sums(hi, lo):
                pe.matmul(ps_s[:, :], ones[:, :], hi, start=True, stop=False)
                return pe.matmul(ps_s[:, :], ones[:, :], lo, start=False, stop=True)

            def scores(s):
                pe.wait_ge(ql_done, s.n(0))
                if s.h == 0:
                    pe.wait_ge(kl_done, s.t + 1)
                for c in range(KT):
                    after(pe, exp_done, s.n(-1, KT, c + 1))
                    for b in range(2):
                        kt = slice((b * KT + c) * P, (b * KT + c + 1) * P)
                        tok = slice(b * N, (b + 1) * N)
                        last = mm3(ps_sim[:, c, tok], k_h[:, kt], k_l[:, kt], q_h[:, tok], q_l[:, tok], True, True)
                    last.then_inc(sim_done, 1)

            def q_norm(s):
                pe.wait_ge(sql_done, s.n(1))
                after(pe, dln_done, s.n(-2))
                if s.h == HEADS - 1 and not s.last:
                    pe.wait_ge(kln_done, s.t + 2)
                column_sums(sq_h[:, :], sq_l[:, :]).then_inc(qsum_done, 1)

            def attend(s):
                pe.wait_ge(pl_done, s.n(-1, KT))
                after(pe, on_done, s.n(-2))
                if s.h == 1:
                    pe.wait_ge(vl_done, s.t + 1)
                par = (s.h - 1) % 2
                for b in range(2):
                    tok = slice(b * N, (b + 1) * N)
                    for c in range(KT):
                        i = b * KT + c
                        last = mm3(ps_o[:, tok], v_h[:, i, :], v_l[:, i, :], pr_h[:, par, c, tok], pr_l[:, par, c, tok],
                                   c == 0, c == KT - 1)
                last.then_inc(av_done, 1)

            def softmax_sums(s):
                pe.wait_ge(ssl_done, s.n(-1))
                if s.has(1):
                    pe.wait_ge(qln_done, s.n(1))
                column_sums(ss_h[:, :], ss_l[:, :]).then_inc(den_done, 1)

            def q_project(s):
                after(pe, qn_done, s.n(1))
                if s.h + 2 == HEADS:
                    pe.wait_ge(xch_done, s.t + 2)
                    pe.wait_ge(xcl_done, s.t + 2)
                h = (s.h + 2) % HEADS
                project(ps_q[:, :], wq_h, wq_l, slice(h * DH, (h + 1) * DH), xc_h, xc_l).then_inc(qproj_done, 1)

            def out_project(s):
                pe.wait_ge(ol_done, s.n(-2))
                if s.h == 2:
                    after(pe, oxa_done, s.t)
                    after(pe, oxd_done, s.t)
                    if s.first:
                        pe.wait_ge(w_lo, 4)
                h = (s.h - 2) % HEADS
                for j in range(TILES):
                    tile = slice(j * P, (j + 1) * P)
                    last = mm3(ps_out[:, j, :], o_h[:, tile], o_l[:, tile], wo_h[:, h, :], wo_l[:, h, :],
                               h == 0 and j % 2 == 0, h == HEADS - 1, skip_group_check=True)
                last.then_inc(out_done, 1)

            def x_transpose(u, c):
                if c == 0:
                    pe.wait_ge(p_ln, u * (2 * LN_OPS) + 2 * LN_OPS)
                else:
                    pe.wait_ge(xnl_done, u * DC + c)
                for i in range(TILES):
                    last = pe.transpose(ps_x[:, i * P:(i + 1) * P], xin[:, i // KT, i % KT, c * P:(c + 1) * P], ident[:, :])
                last.then_inc(xt_tr, 1)

            def k_project(u):
                pe.wait_ge(xnl_done, u * DC + DC)
                project(ps_x[:, :], wkv_h, wkv_l, slice(0, DH), xn_h, xn_l).then_inc(kproj_done, 1)

            def k_norm(u, s):
                pe.wait_ge(ksql_done, u + 1)
                if s is not None:
                    after(pe, dln_done, s.n(-1))
                column_sums(ksq_h[:, :], ksq_l[:, :]).then_inc(ksum_done, 1)

            def v_project(u):
                pe.wait_ge(kn_done, u + 1)
                project(ps_x[:, :], wkv_h, wkv_l, slice(DH, 2 * DH), xn_h, xn_l).then_inc(vproj_done, 1)

            def v_transpose(u):
                pe.wait_ge(vt_done, u + 1)
                for i in range(TILES):
                    last = pe.transpose(ps_x[:, i * P:(i + 1) * P], vt[:, i * P:(i + 1) * P], ident[:, :])
                last.then_inc(vtr_done, 1)

            def h_transpose(w, c):
                if c == 0:
                    pe.wait_ge(e_mod, w * E_MOD + 8)
                    if isinstance(w, int) and w == PAIRS - 1:
                        pe.wait_ge(f_done, w * TILES)
                    else:
                        pe.wait_ge(vl_done, w + 2)
                else:
                    pe.wait_ge(hl_done, w * DC + c)
                for i in range(TILES):
                    last = pe.transpose(ps_x[:, i * P:(i + 1) * P], ox[:, i // KT, i % KT, c * P:(c + 1) * P], ident[:, :])
                last.then_inc(h_tr, 1)

            def up(w, m):
                if m == 0:
                    pe.wait_ge(hl_done, w * DC + DC)
                else:
                    pe.wait_ge(rl_done, w * DC + m)
                project(ps_x[:, :], wup_h, wup_l, slice(m * P, (m + 1) * P), ht_h, ht_l).then_inc(up_done, 1)

            def expert(w, j):
                if j == 0:
                    pe.wait_ge(rl_done, w * DC + DC)
                else:
                    pe.wait_ge(ex_done, w * TILES + j)
                tile = slice(j * P, (j + 1) * P)
                for c in range(DC):
                    last = mm3(ps_x[:, 0:EG], ht_h[:, c, tile], ht_l[:, c, tile], weg_h[:, c, :], weg_l[:, c, :],
                               c == 0, c == DC - 1)
                last.then_inc(xg_done, 1)

            def shared(w, b):
                if b == 0:
                    pe.wait_ge(ex_done, w * TILES + TILES)
                else:
                    pe.wait_ge(f_done, w * TILES + KT)
                for j in range(KT):
                    tile = slice((b * KT + j) * P, (b * KT + j + 1) * P)
                    for c in range(DC):
                        last = mm3(ps_x[:, j * D:(j + 1) * D], rt_h[:, c, tile], rt_l[:, c, tile],
                                   wdn_h[:, c, :], wdn_l[:, c, :], c == 0, c == DC - 1)
                last.then_inc(shared_done, 1)

            def piece_a(s):
                h, t = s.h, s.t
                if not s.first:
                    if h == 7:
                        h_transpose(t - 1, 0)
                    if h == 8:
                        up(t - 1, 0)
                    if h == 9:
                        expert(t - 1, 0)
                    if h == 10:
                        expert(t - 1, 2)
                    if h == 12:
                        shared(t - 1, 1)
                if not s.last:
                    if h == 13:
                        x_transpose(t + 1, 1)
                    if h == 15:
                        v_project(t + 1)

            def piece_b(s):
                h, t = s.h, s.t
                if not s.first:
                    if h == 7:
                        h_transpose(t - 1, 1)
                    if h == 8:
                        up(t - 1, 1)
                    if h == 9:
                        expert(t - 1, 1)
                    if h == 10:
                        expert(t - 1, 3)
                    if h == 11:
                        shared(t - 1, 0)
                if not s.last:
                    if h == 12:
                        if not s.first:
                            pe.wait_ge(f_done, t * TILES)
                        else:
                            pe.wait_ge(vl_done, 1)
                        x_transpose(t + 1, 0)
                    if h == 13:
                        k_project(t + 1)
                    if h == 14:
                        k_norm(t + 1, s)
                    if h == 15:
                        v_transpose(t + 1)

            def step(s):
                scores(s)
                if s.has(-1):
                    attend(s)
                if s.has(1):
                    q_norm(s)
                piece_a(s)
                if s.has(-2):
                    out_project(s)
                if s.has(-1):
                    softmax_sums(s)
                if s.has(2):
                    q_project(s)
                piece_b(s)

            pe.wait_ge(c_chain, 3)
            for n, (place, bank) in enumerate(((pr, ps_sim[:, 0, :]), (q_work, ps_sim[:, 1, :]), (o_work, ps_o[:, :]))):
                pe.wait_ge(wmod_in[n], 16)
                for c in range(DC):
                    last = pe.matmul(bank[0:B, :], c_s[:, c, :], place[:, c, :], start=(c == 0), stop=(c == DC - 1))
                last.then_inc(mod_mm, 1)
            pe.wait_ge(const_done, 1)
            for c in range(DC):
                x_transpose(0, c)
            pe.wait_ge(wkv_lo, 1)
            k_project(0)
            pe.wait_ge(ones_done, 2)
            k_norm(0, None)
            v_project(0)
            v_transpose(0)
            pe.wait_ge(w_lo, 2)
            pe.wait_ge(xch_done, 1)
            pe.wait_ge(xcl_done, 1)
            q_project(START[0])
            pe.wait_ge(kln_done, 1)
            q_norm(START[1])
            q_project(START[1])
            run(pe, step)
            attend(END[0])
            out_project(END[0])
            softmax_sums(END[0])
            out_project(END[1])
            w = PAIRS - 1
            h_transpose(w, 0)
            h_transpose(w, 1)
            up(w, 0)
            up(w, 1)
            for j in range(TILES):
                expert(w, j)
            shared(w, 0)
            shared(w, 1)

        @block.scalar
        def _(act):
            def copy(o, i, **kw):
                return act.activation(o, i, ACT.Copy, **kw)

            def exps(s):
                for c in range(KT):
                    act.wait_ge(sim_done, s.n(0, KT, c + 1))
                    after(act, pl_done, s.n(-1, KT, c + 1))
                    if c == 0:
                        after(act, ss_done, s.n(-1))
                    act.activation(pr[:, c, :], ps_sim[:, c, :], ACT.Exp).then_inc(exp_done, 1)

            def den_recip(s):
                act.wait_ge(den_done, s.n(-1))
                after(act, on_done, s.n(-2))
                act.activation(rden, ps_s[:, :], ACT.Ln, scale=1 / ONE).then_inc(dln_done, 1)
                act.wait_ge(dln_done, s.n(-1))
                act.activation(rden, rden, ACT.Exp, scale=-1.0).then_inc(rden_done, 1)

            def rsqrt(o, i, eps, ln_sem, done_sem, count):
                act.activation(o, i, ACT.Ln, bias=eps[:, :]).then_inc(ln_sem, 1)
                act.wait_ge(ln_sem, count)
                act.activation(o, o, ACT.Exp, scale=-0.5).then_inc(done_sem, 1)

            def q_rsqrt(s):
                act.wait_ge(qsum_done, s.n(1))
                after(act, qn_done, s.n(0))
                rsqrt(rq, ps_s[:, :], eps_q, qln_done, rq_done, s.n(1))

            def ss_hi(s):
                act.wait_ge(ss_done, s.n(0))
                after(act, den_done, s.n(-1))
                copy(ss_h[:, :], ss[:, :]).then_inc(ssh_done, 1)

            def o_hi(s):
                act.wait_ge(on_done, s.n(-2))
                after(act, out_done, s.n(-3))
                copy(o_h[:, :], on).then_inc(oh_done, 1)

            def squares(s):
                act.wait_ge(qproj_done, s.n(1))
                after(act, sql_done, s.n(0))
                act.activation(sq[:, :], ps_q[:, :], ACT.Square).then_inc(sq_done, 1)
                after(act, qsum_done, s.n(0))
                act.activation(sq_h[:, :], ps_q[:, :], ACT.Square).then_inc(sqh_done, 1)

            def xn_hi(u, c):
                act.wait_ge(xt_tr, u * DC + c + 1)
                if c == 0:
                    after(act, vproj_done, u)
                    after(act, xcl_done, u)
                copy(xn_h[:, c, :], ps_x[:, :], scale=gn[:, c:c + 1]).then_inc(xnh_done, 1)

            def x_move(u, s):
                if s is not None:
                    act.wait_ge(qproj_done, s.n(1))
                act.wait_ge(xnh_done, u * DC + DC)
                copy(xc_h[:, :, :], xn_h[:, :, :].bitcast(F32)).then_inc(xch_done, 1)

            def k_squares(u):
                act.wait_ge(kproj_done, u + 1)
                act.activation(ksq, ps_x[:, :], ACT.Square).then_inc(ksq_done, 1)
                act.activation(ksq_h[:, :], ps_x[:, :], ACT.Square).then_inc(ksqh_done, 1)

            def k_rsqrt(u):
                act.wait_ge(ksum_done, u + 1)
                act.wait_ge(ksql_done, u + 1)
                rsqrt(kr, ps_s[:, :], eps_k, kln_done, rk_done, u + 1)

            def ln_rsqrt(ln, ln_sem, ln_count, ln_chain, count):
                _, mv, y0, _, _ = ln
                act.wait_ge(ln_sem, ln_count)
                act.activation(y0[:, :], mv[:, :, 1], ACT.Ln, bias=eps_ln[:, :]).then_inc(ln_chain, 1)
                act.wait_ge(ln_chain, count + 1)
                act.activation(y0[:, :], y0[:, :], ACT.Exp, scale=-0.5).then_inc(ln_chain, 1)

            def p_rsqrt(u, k):
                ln_rsqrt(ln_p, p_ln, u * (2 * LN_OPS) + (k * LN_OPS + 2 * TILES), p_rs, u * 4 + 2 * k)

            def e_rsqrt(w, k):
                ln_rsqrt(ln_e, e_ln, w * (2 * LN_OPS) + (k * LN_OPS + 2 * TILES), e_rs, w * 4 + 2 * k)

            def k_hi(u, s):
                act.wait_ge(kn_done, u + 1)
                if s is not None:
                    act.wait_ge(sim_done, s.n(0, KT))
                copy(k_h[:, :], kn).then_inc(kh_done, 1)

            def v_copy(u):
                act.wait_ge(vproj_done, u + 1)
                act.wait_ge(kn_done, u + 1)
                copy(vt, ps_x[:, :]).then_inc(vt_done, 1)

            def v_hi(u, s):
                act.wait_ge(vtr_done, u + 1)
                if s is not None:
                    after(act, av_done, s.n(-1))
                copy(v_h[:, :, :].rearrange("p i d -> p (i d)"), ps_x[:, :]).then_inc(vh_done, 1)

            def take_out(w, s):
                act.wait_ge(out_done, s.n(-2))
                after(act, out_stored, w * 16)
                copy(ox[:, 0, :, :], ps_out[:, 0:KT, :]).then_inc(oxa_done, 1)

            def h_hi(w, c):
                act.wait_ge(h_tr, w * DC + c + 1)
                if c == 0:
                    after(act, xg_done, w * TILES)
                copy(ht_h[:, c, :], ps_x[:, :]).then_inc(hh_done, 1)

            def relu_hi(w, m):
                act.wait_ge(up_done, w * DC + m + 1)
                if m == 0:
                    after(act, shared_done, w * 2)
                act.activation(rt_h[:, m, :], ps_x[:, :], ACT.Relu).then_inc(rh_done, 1)

            def take_expert(w, j):
                act.wait_ge(xg_done, w * TILES + j + 1)
                if j == 0:
                    after(act, f_done, w * TILES)
                copy(ex[:, j, :], ps_x[:, 0:EG]).then_inc(ex_done, 1)

            def gate_exps(w):
                act.wait_ge(gate, w * GATE + 5)
                act.activation(g_e[:, :, :], g_d[:, :, :], ACT.Exp).then_inc(gate_exp, 1)

            def consume_a(s):
                h, t = s.h, s.t
                if not s.first:
                    if h == 0:
                        v_hi(t, s)
                    if h == 7:
                        h_hi(t - 1, 0)
                    if h == 8:
                        relu_hi(t - 1, 0)
                    if h == 9:
                        take_expert(t - 1, 0)
                    if h == 10:
                        take_expert(t - 1, 2)
                if not s.last:
                    if h == 13:
                        xn_hi(t + 1, 1)
                    if h == 15:
                        v_copy(t + 1)

            def consume_b(s):
                h, t = s.h, s.t
                if not s.first:
                    if h == 1:
                        take_out(t - 1, s)
                    if h == 2:
                        e_rsqrt(t - 1, 0)
                    if h == 4:
                        e_rsqrt(t - 1, 1)
                    if h == 7:
                        h_hi(t - 1, 1)
                    if h == 8:
                        relu_hi(t - 1, 1)
                    if h == 9:
                        take_expert(t - 1, 1)
                    if h == 10:
                        take_expert(t - 1, 3)
                    if h == 11:
                        gate_exps(t - 1)
                if not s.last:
                    if h == 6:
                        p_rsqrt(t + 1, 0)
                    if h == 10:
                        p_rsqrt(t + 1, 1)
                    if h == 12:
                        xn_hi(t + 1, 0)
                    if h == 13:
                        k_squares(t + 1)
                    if h == 14:
                        k_rsqrt(t + 1)

            def step(s):
                if s.has(1):
                    squares(s)
                if s.has(-2):
                    o_hi(s)
                exps(s)
                if s.h == 14 and not s.last:
                    x_move(s.t + 1, s)
                if s.h == 15 and not s.last:
                    k_hi(s.t + 1, s)
                if s.has(1):
                    q_rsqrt(s)
                ss_hi(s)
                consume_a(s)
                if s.has(-1):
                    den_recip(s)
                consume_b(s)

            act.preload_act_table_set("natural_log_exp_and_others")
            act.wait_ge(c_in, 16)
            act.activation(c_e[:, :, :], c_sb[:, :, :], ACT.Exp, scale=-1.0).then_inc(c_exp, 1)
            act.wait_ge(eps_done, 3)
            p_rsqrt(0, 0)
            act.wait_ge(wkv_in, 16)
            copy(wkv_h[:, :, :], ss[:, :].rearrange("p (c n) -> p c n", c=DC)).then_inc(wkv_hi, 1)
            act.wait_ge(stage_in[0], 16)
            copy(wq_h[:, 0, :], late[:, 0, :]).then_inc(w_hi, 1)
            act.wait_ge(stage_in[1], 16)
            copy(wq_h[:, 1, :], late[:, 1, :]).then_inc(w_hi, 1)
            p_rsqrt(0, 1)
            act.wait_ge(gn_in, 16)
            xn_hi(0, 0)
            xn_hi(0, 1)
            x_move(0, None)
            k_squares(0)
            k_rsqrt(0)
            v_copy(0)
            k_hi(0, None)
            v_hi(0, None)
            for i in range(2):
                act.wait_ge(stage_in[i], 32)
                copy(wo_h[:, 8 * i:8 * (i + 1), :], late[:, i, :].rearrange("p (h n) -> p h n", n=D)).then_inc(w_hi, 1)
                if i == 0:
                    squares(START[1])
                    q_rsqrt(START[1])
            run(act, step)
            o_hi(END[0])
            den_recip(END[0])
            o_hi(END[1])
            take_out(PAIRS - 1, END[1])
            e_rsqrt(PAIRS - 1, 0)
            e_rsqrt(PAIRS - 1, 1)
            for c in range(DC):
                h_hi(PAIRS - 1, c)
            for m in range(DC):
                relu_hi(PAIRS - 1, m)
            for j in range(TILES):
                take_expert(PAIRS - 1, j)
            gate_exps(PAIRS - 1)

        @block.vector
        def _(dve):
            def sub(o, a, b):
                return dve.tensor_tensor(o, a, b, ALU.subtract)

            def ln_stats(src, ln, s, base):
                st, mv, _, nf, _ = ln
                for i in range(TILES):
                    dve.bn_stats(st[:, i, :], src[:, i // KT, i % KT, :]).then_inc(s, 1)
                dve.wait_ge(s, base + TILES)
                dve.memset(nf[:, :], 0.0)
                for i in range(TILES):
                    dve.bn_aggr(mv[:, i, :], st[:, i, :]).then_inc(s, 1)

            def ln_apply(src, dst, ln, s, base, guess, guess_count):
                _, mv, y0, nf, rs = ln
                dve.wait_ge(guess, guess_count)
                k = base + 2 * TILES
                dve.scalar_tensor_tensor(nf[:, :], mv[:, :, 1], LN_EPS, y0[:, :], ALU.add, ALU.mult).then_inc(s, 1)
                dve.wait_ge(s, k + 1)
                dve.tensor_tensor(nf[:, :], nf[:, :], y0[:, :], ALU.mult).then_inc(s, 1)
                dve.wait_ge(s, k + 2)
                dve.tensor_scalar(nf[:, :], nf[:, :], -0.5, 1.5, ALU.mult, ALU.add).then_inc(s, 1)
                dve.wait_ge(s, k + 3)
                dve.tensor_tensor(rs[:, :], nf[:, :], y0[:, :], ALU.mult).then_inc(s, 1)
                dve.wait_ge(s, k + 4)
                for i in range(TILES):
                    dve.tensor_scalar(dst[:, i // KT, i % KT, :], src[:, i // KT, i % KT, :], mv[:, i, 0:1], rs[:, i:i + 1],
                                      ALU.subtract, ALU.mult).then_inc(s, 1)

            def q_norms(s):
                dve.wait_ge(rq_done, s.n(1))
                dve.tensor_tensor(qn, ps_q[:, :], rq, ALU.mult).then_inc(qn_done, 1)
                dve.wait_ge(qn_done, s.n(1))
                after(dve, sim_done, s.n(0, KT))
                dve.tensor_copy(q_h[:, :], qn).then_inc(qh_done, 1)

            def sq_lo(s):
                dve.wait_ge(sqh_done, s.n(1))
                sub(sq_l[:, :], sq[:, :], sq_h[:, :].bitcast(F32)).then_inc(sql_done, 1)

            def q_lo(s):
                dve.wait_ge(qh_done, s.n(1))
                sub(q_l[:, :], qn, q_h[:, :].bitcast(F32)).then_inc(ql_done, 1)

            def p_hi(s, c):
                dve.wait_ge(exp_done, s.n(0, KT, c + 1))
                after(dve, av_done, s.n(-2))
                dve.tensor_copy(pr_h[:, s.h % 2, c, :], pr[:, c, :]).then_inc(ph_done, 1)

            def p_lo(s, c):
                dve.wait_ge(ph_done, s.n(0, KT, c + 1))
                sub(pr_l[:, s.h % 2, c, :], pr[:, c, :], pr_h[:, s.h % 2, c, :].bitcast(F32)).then_inc(pl_done, 1)

            def o_norm(s):
                dve.wait_ge(rden_done, s.n(-1))
                dve.wait_ge(av_done, s.n(-1))
                after(dve, oh_done, s.n(-2))
                after(dve, ol_done, s.n(-2))
                dve.tensor_tensor(on, ps_o[:, :], rden, ALU.mult).then_inc(on_done, 1)

            def first_norm(u):
                dve.wait_ge(xin_in, u * 16 + 16)
                ln_stats(xin, ln_p, p_ln, u * (2 * LN_OPS))

            def first_apply(u):
                ln_apply(xin, xin, ln_p, p_ln, u * (2 * LN_OPS), p_rs, u * 4 + 2)

            def second_norm(u):
                dve.wait_ge(p_mod, u * 4 + 4)
                ln_stats(xin, ln_p, p_ln, u * (2 * LN_OPS) + LN_OPS)

            def second_apply(u):
                ln_apply(xin, xin, ln_p, p_ln, u * (2 * LN_OPS) + LN_OPS, p_rs, u * 4 + 4)

            def xn_lo(u, c):
                dve.wait_ge(xnh_done, u * DC + c + 1)
                dve.scalar_tensor_tensor(xn_l[:, c, :], ps_x[:, :], gn[:, c:c + 1], xn_h[:, c, :].bitcast(F32),
                                         ALU.mult, ALU.subtract).then_inc(xnl_done, 1)

            def x_move(u, s):
                if s is not None:
                    dve.wait_ge(qproj_done, s.n(1))
                dve.wait_ge(xnl_done, u * DC + DC)
                dve.tensor_copy(xc_l[:, :, :], xn_l[:, :, :].bitcast(F32)).then_inc(xcl_done, 1)

            def k_norms(u):
                dve.wait_ge(rk_done, u + 1)
                dve.tensor_tensor(kn, ps_x[:, :], kr, ALU.mult).then_inc(kn_done, 1)

            def k_lo(u):
                dve.wait_ge(kh_done, u + 1)
                sub(k_l[:, :], kn, k_h[:, :].bitcast(F32)).then_inc(kl_done, 1)

            def v_lo(u):
                dve.wait_ge(vh_done, u + 1)
                sub(v_l[:, :, :].rearrange("p i d -> p (i d)"), ps_x[:, :],
                    v_h[:, :, :].rearrange("p i d -> p (i d)").bitcast(F32)).then_inc(vl_done, 1)

            def take_out(w, s):
                dve.wait_ge(out_done, s.n(-2))
                after(dve, out_stored, w * 16)
                dve.tensor_copy(ox[:, 1, :, :], ps_out[:, KT:2 * KT, :]).then_inc(oxd_done, 1)

            def third_norm(w):
                dve.wait_ge(oxa_done, w + 1)
                dve.wait_ge(oxd_done, w + 1)
                ln_stats(ox, ln_e, e_ln, w * (2 * LN_OPS))

            def third_apply(w):
                ln_apply(ox, ox, ln_e, e_ln, w * (2 * LN_OPS), e_rs, w * 4 + 2)

            def fourth_norm(w):
                dve.wait_ge(e_mod, w * E_MOD + 4)
                ln_stats(xres, ln_e, e_ln, w * (2 * LN_OPS) + LN_OPS)

            def fourth_apply(w):
                ln_apply(xres, ox, ln_e, e_ln, w * (2 * LN_OPS) + LN_OPS, e_rs, w * 4 + 4)

            def h_lo(w, c):
                dve.wait_ge(hh_done, w * DC + c + 1)
                sub(ht_l[:, c, :], ps_x[:, :], ht_h[:, c, :].bitcast(F32)).then_inc(hl_done, 1)

            def relu_lo(w, m):
                dve.wait_ge(rh_done, w * DC + m + 1)
                dve.scalar_tensor_tensor(rt_l[:, m, :], ps_x[:, :], 0.0, rt_h[:, m, :].bitcast(F32),
                                         ALU.max, ALU.subtract).then_inc(rl_done, 1)

            def gate_top(w):
                dve.wait_ge(ex_done, w * TILES + TILES)
                dve.memset(g_w[:, :], 0.0)
                for j in range(TILES):
                    dve.max(top[:, j, :], ex[:, j, D:EG]).then_inc(gate, 1)
                dve.wait_ge(gate, w * GATE + 4)
                dve.tensor_tensor(g_d[:, :, :], top[:, :, 0:2], top[:, :, 0:1].to_broadcast([P, TILES, 2]),
                                  ALU.subtract).then_inc(gate, 1)

            def gate_weight(w):
                dve.wait_ge(gate_exp, w + 1)
                dve.tensor_tensor(g_s[:, :], g_e[:, :, 0], g_e[:, :, 1], ALU.add).then_inc(gate, 1)
                dve.wait_ge(gate, w * GATE + 6)
                dve.reciprocal(g_i[:, :], g_s[:, :]).then_inc(gate, 1)
                dve.wait_ge(gate, w * GATE + 7)
                dve.tensor_tensor(g_r[:, :, :], g_e[:, :, :], g_i[:, :].unsqueeze(2).to_broadcast([P, TILES, 2]),
                                  ALU.mult).then_inc(gate, 1)
                dve.wait_ge(gate, w * GATE + 8)
                dve.tensor_tensor(g_w[:, :], g_r[:, :, 0], g_r[:, :, 1], ALU.add).then_inc(gate, 1)

            def combine(w, b):
                dve.wait_ge(shared_done, w * 2 + b + 1)
                if b == 0:
                    dve.wait_ge(gate, w * GATE + GATE)
                for j in range(KT):
                    i = b * KT + j
                    dve.scalar_tensor_tensor(ox[:, b, j, :], ex[:, i, 0:D], g_w[:, i:i + 1], ps_x[:, j * D:(j + 1) * D],
                                             ALU.mult, ALU.add).then_inc(f_done, 1)

            def consume_a(s):
                h, t = s.h, s.t
                if not s.first:
                    if h == 0:
                        v_lo(t)
                    if h == 2:
                        third_norm(t - 1)
                    if h == 3:
                        third_apply(t - 1)
                    if h == 5:
                        fourth_apply(t - 1)
                    if h == 7:
                        h_lo(t - 1, 0)
                    if h == 8:
                        relu_lo(t - 1, 0)
                    if h == 12:
                        combine(t - 1, 1)
                if not s.last:
                    if h == 6:
                        first_norm(t + 1)
                    if h == 7:
                        first_apply(t + 1)
                    if h == 10:
                        second_norm(t + 1)
                    if h == 11:
                        second_apply(t + 1)
                    if h == 13:
                        xn_lo(t + 1, 1)

            def consume_b(s):
                h, t = s.h, s.t
                if not s.first:
                    if h == 1:
                        take_out(t - 1, s)
                    if h == 4:
                        fourth_norm(t - 1)
                    if h == 7:
                        h_lo(t - 1, 1)
                    if h == 8:
                        relu_lo(t - 1, 1)
                    if h == 10:
                        gate_top(t - 1)
                    if h == 11:
                        gate_weight(t - 1)
                        combine(t - 1, 0)
                if not s.last:
                    if h == 12:
                        xn_lo(t + 1, 0)
                    if h == 14:
                        k_norms(t + 1)

            def step(s):
                if s.h == 14 and not s.last:
                    x_move(s.t + 1, s)
                if s.has(1):
                    sq_lo(s)
                p_hi(s, 0)
                p_hi(s, 1)
                p_lo(s, 0)
                p_lo(s, 1)
                if s.h == 15 and not s.last:
                    k_lo(s.t + 1)
                if s.has(1):
                    q_norms(s)
                    q_lo(s)
                consume_a(s)
                if s.has(-1):
                    o_norm(s)
                consume_b(s)

            dve.memset(eps_ln[:, :], LN_EPS).then_inc(eps_done, 1)
            dve.memset(eps_q[:, :], L2_EPS / (SCALE * SCALE) * ONE).then_inc(eps_done, 1)
            dve.memset(eps_k[:, :], L2_EPS * ONE).then_inc(eps_done, 1)
            dve.memset(fones, ONE).then_inc(ones_done, 1)
            dve.wait_ge(ones_done, 1)
            dve.tensor_copy(ones[:, :], fones).then_inc(ones_done, 1)
            dve.wait_ge(c_exp, 1)
            dve.tensor_scalar(c_e[:, :, :], c_e[:, :, :], 1.0, None, ALU.add).then_inc(c_chain, 1)
            dve.wait_ge(c_chain, 1)
            dve.reciprocal(c_s[:, :, :], c_e[:, :, :]).then_inc(c_chain, 1)
            dve.wait_ge(c_chain, 2)
            dve.tensor_tensor(c_s[:, :, :], c_sb[:, :, :], c_s[:, :, :], ALU.mult).then_inc(c_chain, 1)
            first_norm(0)
            first_apply(0)
            dve.wait_ge(wkv_hi, 1)
            sub(wkv_l[:, :, :], ss[:, :].rearrange("p (c n) -> p c n", c=DC), wkv_h[:, :, :].bitcast(F32)).then_inc(wkv_lo, 1)
            banks = (ps_sim[0:B, 0, :], ps_sim[0:B, 1, :], ps_o[0:B, :])
            m = mod_a[0:B, :, :, :].rearrange("b e k d -> b (e k) d")
            dve.wait_ge(mod_mm, 3)
            dve.wait_ge(gout_in, 16)
            n_fix = 0

            def row(k):
                return mod_rows[k // 4][:, k % 4, :]

            def fix(ins):
                nonlocal n_fix
                n_fix += 1
                ins.then_inc(mod_fix, 1)
                dve.wait_ge(mod_fix, n_fix)

            fix(dve.tensor_copy(row(0), banks[0][:, 0:D]))
            fix(dve.tensor_scalar(row(1), banks[0][:, D:2 * D], 1.0, None, ALU.add))
            for k, src in ((2, banks[1][:, 0:D]), (5, banks[2][:, D:2 * D])):
                fix(dve.tensor_scalar(m[:, 0, :], src, 0.0, 2.0, ALU.is_ge, ALU.mult))
                fix(dve.scalar_tensor_tensor(m[:, 1, :], m[:, 0, :], -1.0, src, ALU.add, ALU.mult))
                fix(dve.tensor_scalar(m[:, 1, :], m[:, 1, :], 0.25, None, ALU.max))
                fix(dve.scalar_tensor_tensor(row(k), m[:, 0, :], -1.0, m[:, 1, :], ALU.add, ALU.mult))
            fix(dve.tensor_tensor(row(2), row(2), gout16, ALU.mult))
            fix(dve.tensor_copy(row(3), banks[1][:, D:2 * D]))
            fix(dve.tensor_scalar(row(4), banks[2][:, 0:D], 1.0, None, ALU.add))
            assert n_fix == MOD_FIX
            for i in range(2):
                dve.wait_ge(w_hi, i + 1)
                sub(wq_l[:, i, :], late[:, i, :], wq_h[:, i, :].bitcast(F32)).then_inc(w_lo, 1)
            second_norm(0)
            second_apply(0)
            dve.wait_ge(gn_in, 16)
            xn_lo(0, 0)
            xn_lo(0, 1)
            x_move(0, None)
            k_norms(0)
            k_lo(0)
            v_lo(0)
            sq_lo(START[1])
            q_norms(START[1])
            q_lo(START[1])
            for i in range(2):
                dve.wait_ge(w_hi, i + 3)
                sub(wo_l[:, 8 * i:8 * (i + 1), :], late[:, i, :].rearrange("p (h n) -> p h n", n=D),
                    wo_h[:, 8 * i:8 * (i + 1), :].bitcast(F32)).then_inc(w_lo, 1)
            run(dve, step)
            o_norm(END[0])
            w = PAIRS - 1
            take_out(w, END[1])
            third_norm(w)
            third_apply(w)
            fourth_norm(w)
            fourth_apply(w)
            for c in range(DC):
                h_lo(w, c)
            for m_ in range(DC):
                relu_lo(w, m_)
            gate_top(w)
            gate_weight(w)
            combine(w, 0)
            combine(w, 1)

        @block.gpsimd
        def _(pool):
            def tt(o, a, b, op):
                return pool.tensor_tensor(o, a, b, op)

            def rows(m):
                return m.unsqueeze(1).to_broadcast([P, KT, D])

            def p_sum(s):
                pool.wait_ge(exp_done, s.n(0, KT))
                after(pool, ssl_done, s.n(-1))
                tt(ss[:, :], pr[:, 0, :], pr[:, 1, :], ALU.add).then_inc(ss_done, 1)

            def ss_lo(s):
                pool.wait_ge(ssh_done, s.n(0))
                tt(ss_l[:, :], ss[:, :], ss_h[:, :].bitcast(F32), ALU.subtract).then_inc(ssl_done, 1)

            def o_lo(s):
                pool.wait_ge(oh_done, s.n(-2))
                tt(o_l[:, :], on, o_h[:, :].bitcast(F32), ALU.subtract).then_inc(ol_done, 1)

            def modulate_in(u):
                pool.wait_ge(p_ln, u * (2 * LN_OPS) + LN_OPS)
                pool.wait_ge(moda_in, u * 16 + 16)
                for b in range(2):
                    tt(xin[:, b, :, :], xin[:, b, :, :], rows(mod_a[:, b, 1, :]), ALU.mult).then_inc(p_mod, 1)
                for b in range(2):
                    pool.wait_ge(p_mod, u * 4 + (b + 1))
                    tt(xin[:, b, :, :], xin[:, b, :, :], rows(mod_a[:, b, 0, :]), ALU.add).then_inc(p_mod, 1)

            def ksq_lo(u):
                pool.wait_ge(ksqh_done, u + 1)
                tt(ksq_l[:, :], ksq, ksq_h[:, :].bitcast(F32), ALU.subtract).then_inc(ksql_done, 1)

            def residual(w):
                pool.wait_ge(e_ln, w * (2 * LN_OPS) + LN_OPS)
                pool.wait_ge(modb_in, w * 16 + 16)
                pool.wait_ge(xres_in, w * 16 + 16)
                for b in range(2):
                    tt(ox[:, b, :, :], ox[:, b, :, :], rows(mod_b[:, b, 0, :]), ALU.mult).then_inc(e_mod, 1)
                for b in range(2):
                    pool.wait_ge(e_mod, w * E_MOD + (b + 1))
                    tt(xres[:, b, :, :], xres[:, b, :, :], ox[:, b, :, :], ALU.add).then_inc(e_mod, 1)

            def modulate_mlp(w):
                pool.wait_ge(e_ln, w * (2 * LN_OPS) + 2 * LN_OPS)
                for b in range(2):
                    tt(ox[:, b, :, :], ox[:, b, :, :], rows(mod_b[:, b, 2, :]), ALU.mult).then_inc(e_mod, 1)
                for b in range(2):
                    pool.wait_ge(e_mod, w * E_MOD + (4 + b + 1))
                    tt(ox[:, b, :, :], ox[:, b, :, :], rows(mod_b[:, b, 1, :]), ALU.add).then_inc(e_mod, 1)

            def finish(w):
                for b in range(2):
                    pool.wait_ge(f_done, w * TILES + (b + 1) * KT)
                    tt(ox[:, b, :, :], ox[:, b, :, :], rows(mod_b[:, b, 3, :]), ALU.mult).then_inc(e_mod, 1)
                for b in range(2):
                    pool.wait_ge(e_mod, w * E_MOD + (8 + b + 1))
                    tt(ox[:, b, :, :], ox[:, b, :, :], xres[:, b, :, :], ALU.add).then_inc(e_mod, 1)

            def step(s):
                h, t = s.h, s.t
                if s.has(-2):
                    o_lo(s)
                p_sum(s)
                if not s.last and h == 14:
                    ksq_lo(t + 1)
                ss_lo(s)
                if not s.first:
                    if h == 3:
                        residual(t - 1)
                    if h == 5:
                        modulate_mlp(t - 1)
                    if h == 13:
                        finish(t - 1)
                if not s.last and h == 8:
                    modulate_in(t + 1)

            pool.memset(ident[:, :], 0.0).then_inc(const_zero, 1)
            pool.wait_ge(const_zero, 1)
            pool.affine_select(out=ident[:, :], in_=ident[:, :], compare_op=ALU.not_equal, fill=1.0, base=0,
                               pattern=[[-1, P]], channel_multiplier=1).then_inc(const_done, 1)
            pool.wait_ge(mod_fix, MOD_FIX)
            pool.dma_start(scratch[:, 0:4, :], mod_rows[0]).then_inc(mod_stored, 16)
            pool.dma_start(scratch[:, 4:6, :], mod_rows[1]).then_inc(mod_stored, 16)
            modulate_in(0)
            ksq_lo(0)
            def split2(i):
                stage2 = ex[:, :, :].rearrange("p j n -> p (j n)")
                hi, lo, n = ((weg_h, weg_l, EG), (wup_h, wup_l, D), (wdn_h, wdn_l, D))[i]
                src = stage2[:, 0:DC * n].rearrange("p (c n) -> p c n", c=DC)
                pool.wait_ge(w2_in, 32 + 16 * i)
                pool.tensor_copy(hi[:, :, :], src).then_inc(w2_hi, 1)
                pool.wait_ge(w2_hi, i + 1)
                tt(lo[:, :, :], src, hi[:, :, :].bitcast(F32), ALU.subtract).then_inc(w2_lo, 1)

            for i in range(3):
                split2(i)
            run(pool, step)
            o_lo(END[0])
            o_lo(END[1])
            w = PAIRS - 1
            residual(w)
            modulate_mlp(w)
            finish(w)


def kernel(L0_attn_x, L0_attn_g_norm, L0_attn_Wq, L0_attn_Wkv, L0_attn_Wout, L0_attn_g_out, L0_ffn_W_up,
           L0_ffn_W_down, L0_ffn_W_gate, L0_ffn_W_expert, L0_c, L0_wmod):
    import numpy as np
    import concourse.bacc as bacc
    from concourse.bass_utils import run_bass_kernel_spmd

    nc = bacc.Bacc("TRN2", target_bir_lowering=False, num_devices=1)
    arrays = {
        "x": L0_attn_x, "g_norm_pc": np.transpose(np.reshape(L0_attn_g_norm, (DC, P))), "wq": L0_attn_Wq, "wkv": L0_attn_Wkv, "wo": L0_attn_Wout,
        "g_out": L0_attn_g_out, "wup_t": np.transpose(L0_ffn_W_up), "wdown_t": np.transpose(L0_ffn_W_down),
        "wgate_t": np.transpose(L0_ffn_W_gate), "wexp": L0_ffn_W_expert, "c_t": np.transpose(L0_c), "wmod": L0_wmod,
    }
    arrays = {name: np.ascontiguousarray(a) for name, a in arrays.items()}
    args = [nc.dram_tensor(name, a.shape, mybir.dt.from_np(a.dtype), kind="ExternalInput").ap()
            for name, a in arrays.items()]
    scratch = nc.dram_tensor("modulation", (B, 6, D), F32, kind="Internal").ap()
    out = nc.dram_tensor("out", (B, N, D), F32, kind="ExternalOutput").ap()
    adaln_block(nc, *args, scratch, out)
    r = run_bass_kernel_spmd(nc, [arrays], core_ids=[0])
    return r.results[0]["out"]
```

```python
from contextlib import ExitStack

import concourse.bass as bass
from concourse import mybir

F32 = mybir.dt.float32
F32R = mybir.dt.float32r
ALU = mybir.AluOpType
ACT = mybir.ActivationFunctionType


B, N, D = 16, 256, 256
HEADS, DH = 16, 128
P = 128
DC = D // P
PAIRS = B // 2
TOK = 2 * N
KT = N // P
TILES = TOK // P
EXPERTS = 8
EG = D + EXPERTS
LN_EPS = 1e-5
SCALE = 16.0
L2_EPS = 1e-12
ONE = 1.0 / SCALE
NEWTON = 4
P_LN1 = 3 * TILES + NEWTON
P_LN = 2 * P_LN1
P_MOD = 4
E_READY = 2 * TILES + NEWTON + KT
E_LN1 = E_READY + 2 * KT
E_LN = 2 * E_LN1
E_MOD = 8
MOD_FIX = 13
GATE = 4 + 5


def adaln_block(nc, x, g_norm_pc, wq, wkv, wo, g_out, wup_t, wdown_t, wgate_t, wexp, c_t, wmod, scratch, out):
    x_v = x.rearrange("(u b) (j p) d -> u p b j d", b=2, p=P)
    out_v = out.rearrange("(u b) (j p) d -> u p b j d", b=2, p=P)
    mod_v = scratch.rearrange("(u b) k d -> u b k d", b=2)

    with ExitStack() as ctx:
        def sb(name, shape, dt=F32):
            return ctx.enter_context(nc.sbuf_tensor(name, shape, dt))

        def psum(name, shape):
            return ctx.enter_context(nc.psum_tensor(name, shape, F32))

        def sem(name):
            return ctx.enter_context(nc.semaphore(name))

        ps_q = psum("ps_q", [P, TOK])
        ps_s = psum("ps_s", [P, TOK])
        ps_sim = psum("ps_sim", [P, KT, TOK])
        ps_o = psum("ps_o", [P, TOK])
        ps_out = psum("ps_out", [P, TILES, D])
        ps_x = psum("ps_x", [P, TOK])

        wq_h, wq_l = sb("wq_h", [P, DC, HEADS * DH], F32R), sb("wq_l", [P, DC, HEADS * DH], F32R)
        wo_h, wo_l = sb("wo_h", [P, HEADS, D], F32R), sb("wo_l", [P, HEADS, D], F32R)
        wkv_h, wkv_l = sb("wkv_h", [P, DC, 2 * DH], F32R), sb("wkv_l", [P, DC, 2 * DH], F32R)
        wup_h, wup_l = sb("wup_h", [P, DC, D], F32R), sb("wup_l", [P, DC, D], F32R)
        wdn_h, wdn_l = sb("wdn_h", [P, DC, D], F32R), sb("wdn_l", [P, DC, D], F32R)
        weg_h, weg_l = sb("weg_h", [P, DC, EG], F32R), sb("weg_l", [P, DC, EG], F32R)
        ones = sb("ones", [P, P], F32R)
        ident = sb("ident", [P, P])
        gn = sb("gn", [P, DC])

        xn_h, xn_l = sb("xn_h", [P, DC, TOK], F32R), sb("xn_l", [P, DC, TOK], F32R)
        xc_h, xc_l = sb("xc_h", [P, DC, TOK], F32R), sb("xc_l", [P, DC, TOK], F32R)
        k_h, k_l = sb("k_h", [P, TOK], F32R), sb("k_l", [P, TOK], F32R)
        v_h, v_l = sb("v_h", [P, TILES, DH], F32R), sb("v_l", [P, TILES, DH], F32R)
        xin = sb("xin", [P, 2, KT, D])
        xin_flat = xin[:, :, :, :].rearrange("p b j d -> p (b j d)")
        ksq, kn = xin_flat[:, 0:TOK], xin_flat[:, TOK:2 * TOK]
        kr, vt = ksq, ksq
        ksq_h, ksq_l = sb("ksq_h", [P, TOK], F32R), sb("ksq_l", [P, TOK], F32R)
        mod_a = sb("mod_a", [P, 2, 2, D])
        late = sb("late", [P, 2, 2048])
        mod_b = late[:, 0, :].rearrange("p (b k d) -> p b k d", b=2, k=4)
        xres = late[:, 1, 0:1024].rearrange("p (b j d) -> p b j d", b=2, j=KT)
        ox = late[:, 1, 1024:2048].rearrange("p (b j d) -> p b j d", b=2, j=KT)
        ht_h, ht_l = sb("ht_h", [P, DC, TOK], F32R), sb("ht_l", [P, DC, TOK], F32R)
        rt_h, rt_l = sb("rt_h", [P, DC, TOK], F32R), sb("rt_l", [P, DC, TOK], F32R)
        ex = sb("ex", [P, TILES, EG])

        sq = sb("sq", [P, TOK])
        sq_h, sq_l = sb("sq_h", [P, TOK], F32R), sb("sq_l", [P, TOK], F32R)
        fones = sq[:, TOK - P:TOK]
        q_work = sb("q_work", [P, 2, TOK])
        rq, qn = q_work[:, 0, :], q_work[:, 1, :]
        q_h, q_l = sb("q_h", [P, TOK], F32R), sb("q_l", [P, TOK], F32R)
        pr = sb("pr", [P, KT, TOK])
        pr_h, pr_l = sb("pr_h", [P, 2, KT, TOK], F32R), sb("pr_l", [P, 2, KT, TOK], F32R)
        ss = sb("ss", [P, TOK])
        ss_h, ss_l = sb("ss_h", [P, TOK], F32R), sb("ss_l", [P, TOK], F32R)
        o_work = sb("o_work", [P, 2, TOK])
        rden, on = o_work[:, 0, :], o_work[:, 1, :]
        o_h, o_l = sb("o_h", [P, TOK], F32R), sb("o_l", [P, TOK], F32R)

        ln_p = (sb("st_p", [P, TILES, 6]), sb("mv_p", [P, TILES, 2]), sb("y0_p", [P, TILES]), sb("nf_p", [P, TILES]), sb("rs_p", [P, TILES]))
        ln_e = (sb("st_e", [P, TILES, 6]), sb("mv_e", [P, TILES, 2]), sb("y0_e", [P, TILES]), sb("nf_e", [P, TILES]), sb("rs_e", [P, TILES]))
        eps_ln, eps_q, eps_k = sb("eps_ln", [P, 1]), sb("eps_q", [P, 1]), sb("eps_k", [P, 1])
        top = sb("top", [P, TILES, 8])
        g_d, g_e, g_r = sb("g_d", [P, TILES, 2]), sb("g_e", [P, TILES, 2]), sb("g_r", [P, TILES, 2])
        g_s, g_i, g_w = sb("g_s", [P, TILES]), sb("g_i", [P, TILES]), sb("g_w", [P, TILES])
        c_sb, c_e, c_s = sb("c_sb", [P, DC, B]), sb("c_e", [P, DC, B]), sb("c_s", [P, DC, B])
        gout16 = sq[0:B, 0:D]
        mod_rows = (pr[0:B, :, :].rearrange("b c (k d) -> b (c k) d", d=D),
                    q_work[0:B, 0, :].rearrange("b (k d) -> b k d", d=D))

        c_in, gn_in, gout_in = sem("c_in"), sem("gn_in"), sem("gout_in")
        wmod_in = [sem(f"wmod_in{n}") for n in range(3)]
        wkv_in, w2_in = sem("wkv_in"), sem("w2_in")
        stage_in = [sem("stage_in0"), sem("stage_in1")]
        xin_in, moda_in, xres_in, modb_in = sem("xin_in"), sem("moda_in"), sem("xres_in"), sem("modb_in")
        out_stored, mod_stored = sem("out_stored"), sem("mod_stored")
        const_zero, const_done, ones_done, eps_done = sem("const_zero"), sem("const_done"), sem("ones_done"), sem("eps_done")
        w_hi, w_lo = sem("w_hi"), sem("w_lo")
        wkv_hi, wkv_lo = sem("wkv_hi"), sem("wkv_lo")
        w2_hi, w2_lo = sem("w2_hi"), sem("w2_lo")
        c_exp, c_chain, mod_mm, mod_fix = sem("c_exp"), sem("c_chain"), sem("mod_mm"), sem("mod_fix")
        p_ln, p_mod, p_rs = sem("p_ln"), sem("p_mod"), sem("p_rs")
        xt_tr, xnh_done, xnl_done = sem("xt_tr"), sem("xnh_done"), sem("xnl_done")
        xch_done, xcl_done = sem("xch_done"), sem("xcl_done")
        kproj_done, ksq_done, ksqh_done, ksql_done = sem("kproj_done"), sem("ksq_done"), sem("ksqh_done"), sem("ksql_done")
        ksum_done, kln_done, rk_done, kn_done, kh_done, kl_done = sem("ksum_done"), sem("kln_done"), sem("rk_done"), sem("kn_done"), sem("kh_done"), sem("kl_done")
        vproj_done, vt_done, vtr_done, vh_done, vl_done = sem("vproj_done"), sem("vt_done"), sem("vtr_done"), sem("vh_done"), sem("vl_done")
        qproj_done, sq_done, sqh_done, sql_done = sem("qproj_done"), sem("sq_done"), sem("sqh_done"), sem("sql_done")
        qsum_done, qln_done, rq_done, qn_done, qh_done, ql_done = sem("qsum_done"), sem("qln_done"), sem("rq_done"), sem("qn_done"), sem("qh_done"), sem("ql_done")
        sim_done, exp_done, ph_done, pl_done = sem("sim_done"), sem("exp_done"), sem("ph_done"), sem("pl_done")
        ss_done, ssh_done, ssl_done, den_done = sem("ss_done"), sem("ssh_done"), sem("ssl_done"), sem("den_done")
        av_done, dln_done, rden_done, on_done, oh_done, ol_done = sem("av_done"), sem("dln_done"), sem("rden_done"), sem("on_done"), sem("oh_done"), sem("ol_done")
        out_done = sem("out_done")
        oxa_done, oxd_done, e_ln, e_mod, e_rs = sem("oxa_done"), sem("oxd_done"), sem("e_ln"), sem("e_mod"), sem("e_rs")
        h_tr, hh_done, hl_done = sem("h_tr"), sem("hh_done"), sem("hl_done")
        up_done, rh_done, rl_done = sem("up_done"), sem("rh_done"), sem("rl_done")
        xg_done, ex_done, gate, gate_exp = sem("xg_done"), sem("ex_done"), sem("gate"), sem("gate_exp")
        shared_done, f_done = sem("shared_done"), sem("f_done")

        def after(eng, s, value):
            if isinstance(value, int) and value <= 0:
                return
            eng.wait_ge(s, value)

        class Step:

            def __init__(self, t, t16, h, first, last, past=False):
                self.t, self.t16, self.h, self.first, self.last, self.past = t, t16, h, first, last, past

            def n(self, d, per=1, k=None):
                k = per if k is None else k
                base = self.t16 if per == 1 else self.t * (HEADS * per)
                return base + (per * (self.h + d) + k)

            def has(self, d):
                if self.past:
                    return d < 0
                return not (self.first and self.h + d < 0) and not (self.last and self.h + d >= HEADS)

        def run(eng, step):
            for h in range(HEADS):
                step(Step(0, 0, h, True, False))
            with eng.Fori(1, PAIRS - 1) as t:
                t16 = t * HEADS
                for h in range(HEADS):
                    step(Step(t, t16, h, False, False))
            for h in range(HEADS):
                step(Step(PAIRS - 1, (PAIRS - 1) * HEADS, h, False, True))

        END = [Step(PAIRS, PAIRS * HEADS, h, False, True, past=True) for h in range(2)]
        START = [Step(0, 0, h, False, False) for h in (-2, -1)]

        block = ctx.enter_context(nc.Block())

        @block.sync
        def _(sp):
            def load_x(u):
                sp.wait_ge(kl_done, u)
                sp.wait_ge(vtr_done, u)
                sp.dma_start(xin[:, :, :, :], x_v[u]).then_inc(xin_in, 16)
                sp.dma_start(mod_a[:, :, :, :], mod_v[u, :, 0:2, :].partition_broadcast(P)).then_inc(moda_in, 16)

            def load_late(w):
                after(sp, e_mod, w * E_MOD)
                sp.dma_start(mod_b, mod_v[w, :, 2:6, :].partition_broadcast(P)).then_inc(modb_in, 16)
                sp.dma_start(xres, x_v[w]).then_inc(xres_in, 16)

            def store(w):
                sp.wait_ge(e_mod, w * E_MOD + E_MOD)
                sp.dma_start(out_v[w], ox).then_inc(out_stored, 16)

            sp.dma_start(c_sb[:, :, :], c_t.rearrange("(c p) b -> p c b", p=P)).then_inc(c_in, 16)
            sp.dma_start(xin[:, :, :, :], x_v[0]).then_inc(xin_in, 16)
            wmod_v = wmod.rearrange("(c p) n -> p c n", p=P)
            for n, place in enumerate((pr, q_work, o_work)):
                sp.dma_start(place[:, :, :], wmod_v[:, :, n * 512:(n + 1) * 512]).then_inc(wmod_in[n], 16)
            sp.dma_start(gout16, g_out.partition_broadcast(B)).then_inc(gout_in, 16)
            sp.dma_start(gn[:, :], g_norm_pc).then_inc(gn_in, 16)
            sp.dma_start(ss[:, :].rearrange("p (c n) -> p c n", c=DC),
                         wkv.rearrange("(c p) n -> p c n", p=P)).then_inc(wkv_in, 16)
            wq_v = wq.rearrange("(c p) n -> c p n", p=P)
            wo_v = wo.rearrange("(g h p) n -> g p h n", g=2, p=P)
            for i in range(2):
                sp.dma_start(late[:, i, :], wq_v[i]).then_inc(stage_in[i], 16)
            sp.wait_ge(mod_stored, 32)
            sp.dma_start(mod_a[:, :, :, :], mod_v[0, :, 0:2, :].partition_broadcast(P)).then_inc(moda_in, 16)
            for i in range(2):
                sp.wait_ge(w_lo, i + 1)
                sp.dma_start(late[:, i, :].rearrange("p (h n) -> p h n", n=D), wo_v[i]).then_inc(stage_in[i], 16)
            stage2 = ex[:, :, :].rearrange("p j n -> p (j n)")
            for i, w in enumerate((None, wup_t, wdown_t)):
                after(sp, w2_lo, i)
                if w is None:
                    place = stage2[:, 0:DC * EG].rearrange("p (c n) -> p c n", c=DC)
                    sp.dma_start(place[:, :, 0:D], wexp.rearrange("(c p) n -> p c n", p=P)).then_inc(w2_in, 16)
                    sp.dma_start(place[:, :, D:EG], wgate_t.rearrange("(c p) n -> p c n", p=P)).then_inc(w2_in, 16)
                else:
                    sp.dma_start(stage2[:, 0:DC * D].rearrange("p (c n) -> p c n", c=DC),
                                 w.rearrange("(c p) n -> p c n", p=P)).then_inc(w2_in, 16)
            load_x(1)
            sp.wait_ge(w_lo, 4)
            with sp.Fori(1, PAIRS - 1) as t:
                load_late(t - 1)
                load_x(t + 1)
                store(t - 1)
            load_late(PAIRS - 2)
            store(PAIRS - 2)
            load_late(PAIRS - 1)
            store(PAIRS - 1)
            sp.wait_ge(out_stored, 16 * PAIRS)

        @block.tensor
        def _(pe):
            def mm3(o, wh, wl, mh, ml, start, stop, **kw):
                pe.matmul(o, wh, mh, start=start, stop=False, **kw)
                pe.matmul(o, wh, ml, start=False, stop=False, **kw)
                return pe.matmul(o, wl, mh, start=False, stop=stop, **kw)

            def project(o, wh, wl, cols, xh, xl):
                for c in range(DC):
                    last = mm3(o, wh[:, c, cols], wl[:, c, cols], xh[:, c, :], xl[:, c, :], c == 0, c == DC - 1)
                return last

            def column_sums(hi, lo):
                pe.matmul(ps_s[:, :], ones[:, :], hi, start=True, stop=False)
                return pe.matmul(ps_s[:, :], ones[:, :], lo, start=False, stop=True)

            def scores(s):
                pe.wait_ge(ql_done, s.n(0))
                if s.h == 0:
                    pe.wait_ge(kl_done, s.t + 1)
                for c in range(KT):
                    after(pe, exp_done, s.n(-1, KT, c + 1))
                    for b in range(2):
                        kt = slice((b * KT + c) * P, (b * KT + c + 1) * P)
                        tok = slice(b * N, (b + 1) * N)
                        last = mm3(ps_sim[:, c, tok], k_h[:, kt], k_l[:, kt], q_h[:, tok], q_l[:, tok], True, True)
                    last.then_inc(sim_done, 1)

            def q_norm(s):
                pe.wait_ge(sql_done, s.n(1))
                after(pe, dln_done, s.n(-2))
                if s.h == 14 and not s.last:
                    pe.wait_ge(kln_done, s.t + 2)
                column_sums(sq_h[:, :], sq_l[:, :]).then_inc(qsum_done, 1)

            def attend(s):
                pe.wait_ge(pl_done, s.n(-1, KT))
                after(pe, on_done, s.n(-2))
                if s.h == 1:
                    pe.wait_ge(vl_done, s.t + 1)
                par = (s.h - 1) % 2
                for b in range(2):
                    tok = slice(b * N, (b + 1) * N)
                    for c in range(KT):
                        i = b * KT + c
                        last = mm3(ps_o[:, tok], v_h[:, i, :], v_l[:, i, :], pr_h[:, par, c, tok], pr_l[:, par, c, tok],
                                   c == 0, c == KT - 1)
                last.then_inc(av_done, 1)

            def softmax_sums(s):
                pe.wait_ge(ssl_done, s.n(-1))
                if s.has(1):
                    pe.wait_ge(qln_done, s.n(1))
                column_sums(ss_h[:, :], ss_l[:, :]).then_inc(den_done, 1)

            def q_project(s):
                after(pe, qn_done, s.n(1))
                if s.h + 2 == HEADS:
                    pe.wait_ge(xch_done, s.t + 2)
                    pe.wait_ge(xcl_done, s.t + 2)
                h = (s.h + 2) % HEADS
                project(ps_q[:, :], wq_h, wq_l, slice(h * DH, (h + 1) * DH), xc_h, xc_l).then_inc(qproj_done, 1)

            def out_project(s):
                pe.wait_ge(ol_done, s.n(-2))
                if s.h == 2:
                    after(pe, oxa_done, s.t)
                    after(pe, oxd_done, s.t)
                    if s.first:
                        pe.wait_ge(w_lo, 4)
                h = (s.h - 2) % HEADS
                for j in range(TILES):
                    tile = slice(j * P, (j + 1) * P)
                    last = mm3(ps_out[:, j, :], o_h[:, tile], o_l[:, tile], wo_h[:, h, :], wo_l[:, h, :],
                               h == 0 and j % 2 == 0, h == HEADS - 1, skip_group_check=True)
                last.then_inc(out_done, 1)

            def x_transpose(u, c, first):
                if c == 0:
                    pe.wait_ge(p_ln, u * P_LN + P_LN)
                if isinstance(u, int) and u == 0:
                    after(pe, xnl_done, c)
                elif first:
                    pe.wait_ge(xnl_done, u * DC + c) if c else pe.wait_ge(vl_done, u)
                else:
                    pe.wait_ge(f_done, (u - 1) * TILES) if c else pe.wait_ge(ex_done, (u - 1) * TILES)
                for i in range(TILES):
                    last = pe.transpose(ps_x[:, i * P:(i + 1) * P], xin[:, i // KT, i % KT, c * P:(c + 1) * P], ident[:, :])
                last.then_inc(xt_tr, 1)

            def k_project(u):
                pe.wait_ge(xnl_done, u * DC + DC)
                project(ps_x[:, :], wkv_h, wkv_l, slice(0, DH), xn_h, xn_l).then_inc(kproj_done, 1)

            def k_norm(u, s):
                pe.wait_ge(ksql_done, u + 1)
                if s is not None:
                    after(pe, dln_done, s.n(-1))
                column_sums(ksq_h[:, :], ksq_l[:, :]).then_inc(ksum_done, 1)

            def v_project(u):
                pe.wait_ge(kn_done, u + 1)
                project(ps_x[:, :], wkv_h, wkv_l, slice(DH, 2 * DH), xn_h, xn_l).then_inc(vproj_done, 1)

            def v_transpose(u):
                pe.wait_ge(vt_done, u + 1)
                for i in range(TILES):
                    last = pe.transpose(ps_x[:, i * P:(i + 1) * P], vt[:, i * P:(i + 1) * P], ident[:, :])
                last.then_inc(vtr_done, 1)

            def h_transpose(w, c):
                if c == 0:
                    pe.wait_ge(e_ln, w * E_LN + E_LN)
                    pe.wait_ge(e_mod, w * E_MOD + 4)
                    if isinstance(w, int) and w == PAIRS - 1:
                        pe.wait_ge(f_done, w * TILES)
                    else:
                        pe.wait_ge(vl_done, w + 2)
                else:
                    pe.wait_ge(hl_done, w * DC + c)
                for i in range(TILES):
                    last = pe.transpose(ps_x[:, i * P:(i + 1) * P], ox[:, i // KT, i % KT, c * P:(c + 1) * P], ident[:, :])
                last.then_inc(h_tr, 1)

            def up(w, m):
                if m == 0:
                    pe.wait_ge(hl_done, w * DC + DC)
                else:
                    pe.wait_ge(rl_done, w * DC + m)
                project(ps_x[:, :], wup_h, wup_l, slice(m * P, (m + 1) * P), ht_h, ht_l).then_inc(up_done, 1)

            def expert(w, j):
                if j == 0:
                    pe.wait_ge(rl_done, w * DC + DC)
                else:
                    pe.wait_ge(ex_done, w * TILES + j)
                tile = slice(j * P, (j + 1) * P)
                for c in range(DC):
                    last = mm3(ps_x[:, 0:EG], ht_h[:, c, tile], ht_l[:, c, tile], weg_h[:, c, :], weg_l[:, c, :],
                               c == 0, c == DC - 1)
                last.then_inc(xg_done, 1)

            def shared(w, b, last):
                if b == 0 and last:
                    pe.wait_ge(ex_done, w * TILES + TILES)
                elif b == 0:
                    pe.wait_ge(xnl_done, (w + 2) * DC + 1)
                else:
                    pe.wait_ge(f_done, w * TILES + KT)
                for j in range(KT):
                    tile = slice((b * KT + j) * P, (b * KT + j + 1) * P)
                    for c in range(DC):
                        last = mm3(ps_x[:, j * D:(j + 1) * D], rt_h[:, c, tile], rt_l[:, c, tile],
                                   wdn_h[:, c, :], wdn_l[:, c, :], c == 0, c == DC - 1)
                last.then_inc(shared_done, 1)

            def piece_a(s):
                h, t = s.h, s.t
                if not s.first:
                    if h == 6:
                        h_transpose(t - 1, 0)
                    if h == 7:
                        up(t - 1, 0)
                    if h == 8:
                        expert(t - 1, 0)
                    if h == 9:
                        expert(t - 1, 2)
                    if h == 11:
                        shared(t - 1, 0, s.last)
                if not s.last:
                    if h == 10:
                        x_transpose(t + 1, 0, s.first)
                    if h == 12:
                        x_transpose(t + 1, 1, s.first)
                    if h == 15:
                        v_transpose(t + 1)

            def piece_b(s):
                h, t = s.h, s.t
                if not s.first:
                    if h == 6:
                        h_transpose(t - 1, 1)
                    if h == 7:
                        up(t - 1, 1)
                    if h == 8:
                        expert(t - 1, 1)
                    if h == 9:
                        expert(t - 1, 3)
                    if h == 11:
                        shared(t - 1, 1, s.last)
                if not s.last:
                    if h == 12:
                        k_project(t + 1)
                    if h == 13:
                        k_norm(t + 1, s)
                    if h == 14:
                        v_project(t + 1)

            def step(s):
                scores(s)
                if s.has(-1):
                    attend(s)
                if s.has(1):
                    q_norm(s)
                piece_a(s)
                if s.has(-2):
                    out_project(s)
                if s.has(-1):
                    softmax_sums(s)
                if s.has(2):
                    q_project(s)
                piece_b(s)

            pe.wait_ge(c_chain, 3)
            for n, (place, bank) in enumerate(((pr, ps_sim[:, 0, :]), (q_work, ps_sim[:, 1, :]), (o_work, ps_o[:, :]))):
                pe.wait_ge(wmod_in[n], 16)
                for c in range(DC):
                    last = pe.matmul(bank[0:B, :], c_s[:, c, :], place[:, c, :], start=(c == 0), stop=(c == DC - 1))
                last.then_inc(mod_mm, 1)
            pe.wait_ge(const_done, 1)
            for c in range(DC):
                x_transpose(0, c, True)
            pe.wait_ge(wkv_lo, 1)
            k_project(0)
            pe.wait_ge(ones_done, 2)
            k_norm(0, None)
            v_project(0)
            v_transpose(0)
            pe.wait_ge(w_lo, 2)
            pe.wait_ge(xch_done, 1)
            pe.wait_ge(xcl_done, 1)
            q_project(START[0])
            pe.wait_ge(kln_done, 1)
            q_norm(START[1])
            q_project(START[1])
            run(pe, step)
            attend(END[0])
            out_project(END[0])
            softmax_sums(END[0])
            out_project(END[1])
            w = PAIRS - 1
            h_transpose(w, 0)
            h_transpose(w, 1)
            up(w, 0)
            up(w, 1)
            for j in range(TILES):
                expert(w, j)
            shared(w, 0, True)
            shared(w, 1, True)

        @block.scalar
        def _(act):
            def copy(o, i, **kw):
                return act.activation(o, i, ACT.Copy, **kw)

            def exps(s):
                for c in range(KT):
                    act.wait_ge(sim_done, s.n(0, KT, c + 1))
                    after(act, pl_done, s.n(-1, KT, c + 1))
                    if c == 0:
                        after(act, ss_done, s.n(-1))
                    act.activation(pr[:, c, :], ps_sim[:, c, :], ACT.Exp).then_inc(exp_done, 1)

            def den_recip(s):
                act.wait_ge(den_done, s.n(-1))
                after(act, on_done, s.n(-2))
                act.activation(rden, ps_s[:, :], ACT.Ln, scale=1 / ONE).then_inc(dln_done, 1)
                act.wait_ge(dln_done, s.n(-1))
                act.activation(rden, rden, ACT.Exp, scale=-1.0).then_inc(rden_done, 1)

            def rsqrt(o, i, eps, ln_sem, done_sem, count):
                act.activation(o, i, ACT.Ln, bias=eps[:, :]).then_inc(ln_sem, 1)
                act.wait_ge(ln_sem, count)
                act.activation(o, o, ACT.Exp, scale=-0.5).then_inc(done_sem, 1)

            def q_rsqrt(s):
                act.wait_ge(qsum_done, s.n(1))
                after(act, qn_done, s.n(0))
                rsqrt(rq, ps_s[:, :], eps_q, qln_done, rq_done, s.n(1))

            def ss_hi(s):
                act.wait_ge(ss_done, s.n(0))
                after(act, den_done, s.n(-1))
                copy(ss_h[:, :], ss[:, :]).then_inc(ssh_done, 1)

            def o_hi(s):
                act.wait_ge(on_done, s.n(-2))
                after(act, out_done, s.n(-3))
                copy(o_h[:, :], on).then_inc(oh_done, 1)

            def squares(s):
                act.wait_ge(qproj_done, s.n(1))
                after(act, sql_done, s.n(0))
                act.activation(sq[:, :], ps_q[:, :], ACT.Square).then_inc(sq_done, 1)
                after(act, qsum_done, s.n(0))
                act.activation(sq_h[:, :], ps_q[:, :], ACT.Square).then_inc(sqh_done, 1)

            def xn_hi(u, c):
                act.wait_ge(xt_tr, u * DC + c + 1)
                if c == 0:
                    after(act, vproj_done, u)
                    after(act, xcl_done, u)
                copy(xn_h[:, c, :], ps_x[:, :], scale=gn[:, c:c + 1]).then_inc(xnh_done, 1)

            def x_move(u, s):
                if s is not None:
                    act.wait_ge(qproj_done, s.n(1))
                act.wait_ge(xnh_done, u * DC + DC)
                copy(xc_h[:, :, :], xn_h[:, :, :].bitcast(F32)).then_inc(xch_done, 1)

            def k_squares(u):
                act.wait_ge(kproj_done, u + 1)
                act.activation(ksq, ps_x[:, :], ACT.Square).then_inc(ksq_done, 1)
                act.activation(ksq_h[:, :], ps_x[:, :], ACT.Square).then_inc(ksqh_done, 1)

            def k_rsqrt(u):
                act.wait_ge(ksum_done, u + 1)
                act.wait_ge(ksql_done, u + 1)
                rsqrt(kr, ps_s[:, :], eps_k, kln_done, rk_done, u + 1)

            def ln_rsqrt(ln, ln_sem, ln_count, ln_chain, count):
                _, mv, y0, _, _ = ln
                act.wait_ge(ln_sem, ln_count)
                act.activation(y0[:, :], mv[:, :, 1], ACT.Ln, bias=eps_ln[:, :]).then_inc(ln_chain, 1)
                act.wait_ge(ln_chain, count + 1)
                act.activation(y0[:, :], y0[:, :], ACT.Exp, scale=-0.5).then_inc(ln_chain, 1)

            def p_rsqrt(u, k):
                ln_rsqrt(ln_p, p_ln, u * P_LN + (k * P_LN1 + 2 * TILES), p_rs, u * 4 + 2 * k)

            def e_rsqrt(w, k):
                ln_rsqrt(ln_e, e_ln, w * E_LN + (k * E_LN1 + 2 * TILES), e_rs, w * 4 + 2 * k)

            def k_hi(u, s):
                act.wait_ge(kn_done, u + 1)
                if s is not None:
                    act.wait_ge(sim_done, s.n(0, KT))
                copy(k_h[:, :], kn).then_inc(kh_done, 1)

            def v_copy(u):
                act.wait_ge(vproj_done, u + 1)
                act.wait_ge(kn_done, u + 1)
                copy(vt, ps_x[:, :]).then_inc(vt_done, 1)

            def v_hi(u, s):
                act.wait_ge(vtr_done, u + 1)
                if s is not None:
                    after(act, av_done, s.n(-1))
                copy(v_h[:, :, :].rearrange("p i d -> p (i d)"), ps_x[:, :]).then_inc(vh_done, 1)

            def take_out(w, s):
                act.wait_ge(out_done, s.n(-2))
                after(act, out_stored, w * 16)
                copy(ox[:, 0, :, :], ps_out[:, 0:KT, :]).then_inc(oxa_done, 1)

            def h_hi(w, c):
                act.wait_ge(h_tr, w * DC + c + 1)
                if c == 0:
                    after(act, xg_done, w * TILES)
                copy(ht_h[:, c, :], ps_x[:, :]).then_inc(hh_done, 1)

            def relu_hi(w, m):
                act.wait_ge(up_done, w * DC + m + 1)
                if m == 0:
                    after(act, shared_done, w * 2)
                act.activation(rt_h[:, m, :], ps_x[:, :], ACT.Relu).then_inc(rh_done, 1)

            def take_expert(w, j):
                act.wait_ge(xg_done, w * TILES + j + 1)
                if j == 0:
                    after(act, f_done, w * TILES)
                copy(ex[:, j, :], ps_x[:, 0:EG]).then_inc(ex_done, 1)

            def gate_exps(w):
                act.wait_ge(gate, w * GATE + 5)
                act.activation(g_e[:, :, :], g_d[:, :, :], ACT.Exp).then_inc(gate_exp, 1)

            def consume_a(s):
                h, t = s.h, s.t
                if not s.first:
                    if h == 0:
                        v_hi(t, s)
                    if h == 6:
                        h_hi(t - 1, 0)
                    if h == 7:
                        relu_hi(t - 1, 0)
                    if h == 8:
                        take_expert(t - 1, 0)
                    if h == 9:
                        take_expert(t - 1, 2)
                if not s.last:
                    if h == 10:
                        xn_hi(t + 1, 0)
                    if h == 12:
                        xn_hi(t + 1, 1)

            def consume_b(s):
                h, t = s.h, s.t
                if not s.first:
                    if h == 1:
                        take_out(t - 1, s)
                    if h == 6:
                        h_hi(t - 1, 1)
                    if h == 7:
                        relu_hi(t - 1, 1)
                    if h == 8:
                        take_expert(t - 1, 1)
                    if h == 9:
                        take_expert(t - 1, 3)
                    if h == 10:
                        gate_exps(t - 1)
                if not s.last:
                    if h == 12:
                        k_squares(t + 1)
                    if h == 13:
                        k_rsqrt(t + 1)
                    if h == 14:
                        v_copy(t + 1)

            def guesses(s):
                if not s.last:
                    if s.h == 2:
                        p_rsqrt(s.t + 1, 0)
                    if s.h == 8:
                        p_rsqrt(s.t + 1, 1)
                if not s.first:
                    if s.h == 3:
                        e_rsqrt(s.t - 1, 0)
                    if s.h == 5:
                        e_rsqrt(s.t - 1, 1)

            def step(s):
                if s.has(1):
                    squares(s)
                if s.has(-2):
                    o_hi(s)
                exps(s)
                if s.h == 14 and not s.last:
                    x_move(s.t + 1, s)
                if s.h == 15 and not s.last:
                    k_hi(s.t + 1, s)
                if s.has(1):
                    q_rsqrt(s)
                guesses(s)
                ss_hi(s)
                consume_a(s)
                if s.has(-1):
                    den_recip(s)
                consume_b(s)

            act.preload_act_table_set("natural_log_exp_and_others")
            act.wait_ge(c_in, 16)
            act.activation(c_e[:, :, :], c_sb[:, :, :], ACT.Exp, scale=-1.0).then_inc(c_exp, 1)
            act.wait_ge(eps_done, 3)
            p_rsqrt(0, 0)
            act.wait_ge(wkv_in, 16)
            copy(wkv_h[:, :, :], ss[:, :].rearrange("p (c n) -> p c n", c=DC)).then_inc(wkv_hi, 1)
            act.wait_ge(stage_in[0], 16)
            copy(wq_h[:, 0, :], late[:, 0, :]).then_inc(w_hi, 1)
            act.wait_ge(stage_in[1], 16)
            copy(wq_h[:, 1, :], late[:, 1, :]).then_inc(w_hi, 1)
            p_rsqrt(0, 1)
            act.wait_ge(gn_in, 16)
            xn_hi(0, 0)
            xn_hi(0, 1)
            x_move(0, None)
            k_squares(0)
            k_rsqrt(0)
            v_copy(0)
            k_hi(0, None)
            v_hi(0, None)
            for i in range(2):
                act.wait_ge(stage_in[i], 32)
                copy(wo_h[:, 8 * i:8 * (i + 1), :], late[:, i, :].rearrange("p (h n) -> p h n", n=D)).then_inc(w_hi, 1)
                if i == 0:
                    squares(START[1])
                    q_rsqrt(START[1])
            run(act, step)
            o_hi(END[0])
            den_recip(END[0])
            o_hi(END[1])
            take_out(PAIRS - 1, END[1])
            e_rsqrt(PAIRS - 1, 0)
            e_rsqrt(PAIRS - 1, 1)
            for c in range(DC):
                h_hi(PAIRS - 1, c)
            for m in range(DC):
                relu_hi(PAIRS - 1, m)
            for j in range(TILES):
                take_expert(PAIRS - 1, j)
            gate_exps(PAIRS - 1)

        @block.vector
        def _(dve):
            def sub(o, a, b):
                return dve.tensor_tensor(o, a, b, ALU.subtract)

            def ln_stats(src, b, ln, s, base):
                st, mv, _, nf, _ = ln
                base += 2 * KT * b
                for i in range(b * KT, (b + 1) * KT):
                    dve.bn_stats(st[:, i, :], src[:, b, i % KT, :]).then_inc(s, 1)
                dve.wait_ge(s, base + KT)
                dve.memset(nf[:, :], 0.0)
                for i in range(b * KT, (b + 1) * KT):
                    dve.bn_aggr(mv[:, i, :], st[:, i, :]).then_inc(s, 1)

            def newton(ln, s, k, guess, guess_count):
                _, mv, y0, nf, rs = ln
                dve.wait_ge(guess, guess_count)
                dve.scalar_tensor_tensor(nf[:, :], mv[:, :, 1], LN_EPS, y0[:, :], ALU.add, ALU.mult).then_inc(s, 1)
                dve.wait_ge(s, k + 1)
                dve.tensor_tensor(nf[:, :], nf[:, :], y0[:, :], ALU.mult).then_inc(s, 1)
                dve.wait_ge(s, k + 2)
                dve.tensor_scalar(nf[:, :], nf[:, :], -0.5, 1.5, ALU.mult, ALU.add).then_inc(s, 1)
                dve.wait_ge(s, k + 3)
                dve.tensor_tensor(rs[:, :], nf[:, :], y0[:, :], ALU.mult).then_inc(s, 1)
                dve.wait_ge(s, k + 4)

            def normal_tile(dst, src, ln, i):
                return dve.tensor_scalar(dst, src, ln[1][:, i, 0:1], ln[4][:, i:i + 1], ALU.subtract, ALU.mult)

            def scale_tile(dst, src, ln, i, m):
                return dve.scalar_tensor_tensor(dst, src, ln[1][:, i, 0:1], m, ALU.subtract, ALU.mult)

            def shift_tile(dst, src, ln, i, m):
                return dve.scalar_tensor_tensor(dst, src, ln[4][:, i:i + 1], m, ALU.mult, ALU.add)

            def q_norms(s):
                dve.wait_ge(rq_done, s.n(1))
                dve.tensor_tensor(qn, ps_q[:, :], rq, ALU.mult).then_inc(qn_done, 1)
                dve.wait_ge(qn_done, s.n(1))
                after(dve, sim_done, s.n(0, KT))
                dve.tensor_copy(q_h[:, :], qn).then_inc(qh_done, 1)

            def sq_lo(s):
                dve.wait_ge(sqh_done, s.n(1))
                sub(sq_l[:, :], sq[:, :], sq_h[:, :].bitcast(F32)).then_inc(sql_done, 1)

            def q_lo(s):
                dve.wait_ge(qh_done, s.n(1))
                sub(q_l[:, :], qn, q_h[:, :].bitcast(F32)).then_inc(ql_done, 1)

            def p_hi(s, c):
                dve.wait_ge(exp_done, s.n(0, KT, c + 1))
                after(dve, av_done, s.n(-2))
                dve.tensor_copy(pr_h[:, s.h % 2, c, :], pr[:, c, :]).then_inc(ph_done, 1)

            def p_lo(s, c):
                dve.wait_ge(ph_done, s.n(0, KT, c + 1))
                sub(pr_l[:, s.h % 2, c, :], pr[:, c, :], pr_h[:, s.h % 2, c, :].bitcast(F32)).then_inc(pl_done, 1)

            def o_norm(s):
                dve.wait_ge(rden_done, s.n(-1))
                dve.wait_ge(av_done, s.n(-1))
                after(dve, oh_done, s.n(-2))
                after(dve, ol_done, s.n(-2))
                dve.tensor_tensor(on, ps_o[:, :], rden, ALU.mult).then_inc(on_done, 1)

            def first_norm(u, b):
                dve.wait_ge(xin_in, u * 16 + 16)
                ln_stats(xin, b, ln_p, p_ln, u * P_LN)

            def first_newton(u):
                newton(ln_p, p_ln, u * P_LN + 2 * TILES, p_rs, u * 4 + 2)

            def p_apply(u, b):
                for i in range(b * KT, (b + 1) * KT):
                    normal_tile(xin[:, b, i % KT, :], xin[:, b, i % KT, :], ln_p, i).then_inc(p_ln, 1)

            def second_norm(u, b):
                dve.wait_ge(p_mod, u * P_MOD + P_MOD)
                ln_stats(xin, b, ln_p, p_ln, u * P_LN + P_LN1)

            def second_newton(u):
                newton(ln_p, p_ln, u * P_LN + P_LN1 + 2 * TILES, p_rs, u * 4 + 4)

            def xn_lo(u, c):
                dve.wait_ge(xnh_done, u * DC + c + 1)
                dve.scalar_tensor_tensor(xn_l[:, c, :], ps_x[:, :], gn[:, c:c + 1], xn_h[:, c, :].bitcast(F32),
                                         ALU.mult, ALU.subtract).then_inc(xnl_done, 1)

            def x_move(u, s):
                if s is not None:
                    dve.wait_ge(qproj_done, s.n(1))
                dve.wait_ge(xnl_done, u * DC + DC)
                dve.tensor_copy(xc_l[:, :, :], xn_l[:, :, :].bitcast(F32)).then_inc(xcl_done, 1)

            def k_norms(u):
                dve.wait_ge(rk_done, u + 1)
                dve.tensor_tensor(kn, ps_x[:, :], kr, ALU.mult).then_inc(kn_done, 1)

            def k_lo(u):
                dve.wait_ge(kh_done, u + 1)
                sub(k_l[:, :], kn, k_h[:, :].bitcast(F32)).then_inc(kl_done, 1)

            def v_lo(u):
                dve.wait_ge(vh_done, u + 1)
                sub(v_l[:, :, :].rearrange("p i d -> p (i d)"), ps_x[:, :],
                    v_h[:, :, :].rearrange("p i d -> p (i d)").bitcast(F32)).then_inc(vl_done, 1)

            def take_out(w, s):
                dve.wait_ge(out_done, s.n(-2))
                after(dve, out_stored, w * 16)
                dve.tensor_copy(ox[:, 1, :, :], ps_out[:, KT:2 * KT, :]).then_inc(oxd_done, 1)

            def third_norm(w, b):
                dve.wait_ge(oxd_done if b else oxa_done, w + 1)
                ln_stats(ox, b, ln_e, e_ln, w * E_LN)

            def third_newton(w):
                newton(ln_e, e_ln, w * E_LN + 2 * TILES, e_rs, w * 4 + 2)
                for j in range(KT):
                    normal_tile(ox[:, 1, j, :], ox[:, 1, j, :], ln_e, KT + j).then_inc(e_ln, 1)

            def third_apply(w):
                dve.wait_ge(modb_in, w * 16 + 16)
                dve.wait_ge(xres_in, w * 16 + 16)
                for j in range(KT):
                    scale_tile(ox[:, 0, j, :], ox[:, 0, j, :], ln_e, j, mod_b[:, 0, 0, :]).then_inc(e_ln, 1)
                dve.wait_ge(e_ln, w * E_LN + E_READY + KT)
                for j in range(KT):
                    shift_tile(xres[:, 0, j, :], ox[:, 0, j, :], ln_e, j, xres[:, 0, j, :]).then_inc(e_ln, 1)

            def fourth_norm(w, b):
                if b == 0:
                    dve.wait_ge(e_ln, w * E_LN + E_LN1)
                else:
                    dve.wait_ge(e_mod, w * E_MOD + 2)
                ln_stats(xres, b, ln_e, e_ln, w * E_LN + E_LN1)

            def fourth_newton(w):
                newton(ln_e, e_ln, w * E_LN + E_LN1 + 2 * TILES, e_rs, w * 4 + 4)
                for j in range(KT):
                    normal_tile(ox[:, 1, j, :], xres[:, 1, j, :], ln_e, KT + j).then_inc(e_ln, 1)

            def fourth_apply(w):
                for j in range(KT):
                    scale_tile(ox[:, 0, j, :], xres[:, 0, j, :], ln_e, j, mod_b[:, 0, 2, :]).then_inc(e_ln, 1)
                dve.wait_ge(e_ln, w * E_LN + E_LN1 + E_READY + KT)
                for j in range(KT):
                    shift_tile(ox[:, 0, j, :], ox[:, 0, j, :], ln_e, j, mod_b[:, 0, 1, :]).then_inc(e_ln, 1)

            def h_lo(w, c):
                dve.wait_ge(hh_done, w * DC + c + 1)
                sub(ht_l[:, c, :], ps_x[:, :], ht_h[:, c, :].bitcast(F32)).then_inc(hl_done, 1)

            def relu_lo(w, m):
                dve.wait_ge(rh_done, w * DC + m + 1)
                dve.scalar_tensor_tensor(rt_l[:, m, :], ps_x[:, :], 0.0, rt_h[:, m, :].bitcast(F32),
                                         ALU.max, ALU.subtract).then_inc(rl_done, 1)

            def gate_top(w):
                dve.wait_ge(ex_done, w * TILES + TILES)
                dve.memset(g_w[:, :], 0.0)
                for j in range(TILES):
                    dve.max(top[:, j, :], ex[:, j, D:EG]).then_inc(gate, 1)
                dve.wait_ge(gate, w * GATE + 4)
                dve.tensor_tensor(g_d[:, :, :], top[:, :, 0:2], top[:, :, 0:1].to_broadcast([P, TILES, 2]),
                                  ALU.subtract).then_inc(gate, 1)

            def gate_weight(w):
                dve.wait_ge(gate_exp, w + 1)
                dve.tensor_tensor(g_s[:, :], g_e[:, :, 0], g_e[:, :, 1], ALU.add).then_inc(gate, 1)
                dve.wait_ge(gate, w * GATE + 6)
                dve.reciprocal(g_i[:, :], g_s[:, :]).then_inc(gate, 1)
                dve.wait_ge(gate, w * GATE + 7)
                dve.tensor_tensor(g_r[:, :, :], g_e[:, :, :], g_i[:, :].unsqueeze(2).to_broadcast([P, TILES, 2]),
                                  ALU.mult).then_inc(gate, 1)
                dve.wait_ge(gate, w * GATE + 8)
                dve.tensor_tensor(g_w[:, :], g_r[:, :, 0], g_r[:, :, 1], ALU.add).then_inc(gate, 1)

            def combine(w, b):
                dve.wait_ge(shared_done, w * 2 + b + 1)
                if b == 0:
                    dve.wait_ge(gate, w * GATE + GATE)
                for j in range(KT):
                    i = b * KT + j
                    dve.scalar_tensor_tensor(ox[:, b, j, :], ex[:, i, 0:D], g_w[:, i:i + 1], ps_x[:, j * D:(j + 1) * D],
                                             ALU.mult, ALU.add).then_inc(f_done, 1)

            def consume_a(s):
                h, t = s.h, s.t
                if not s.first:
                    if h == 0:
                        v_lo(t)
                if not s.last:
                    if h == 1:
                        first_norm(t + 1, 1)
                    if h == 2:
                        first_newton(t + 1)
                        p_apply(t + 1, 0)
                    if h == 8:
                        second_newton(t + 1)
                        p_apply(t + 1, 0)
                    if h == 9:
                        p_apply(t + 1, 1)
                    if h == 10:
                        xn_lo(t + 1, 0)
                    if h == 12:
                        xn_lo(t + 1, 1)
                    if h == 14:
                        k_norms(t + 1)
                if not s.first:
                    if h == 2:
                        third_norm(t - 1, 0)
                    if h == 3:
                        third_newton(t - 1)
                    if h == 4:
                        fourth_norm(t - 1, 0)
                    if h == 5:
                        fourth_newton(t - 1)
                    if h == 6:
                        h_lo(t - 1, 0)
                    if h == 7:
                        relu_lo(t - 1, 0)
                    if h == 10:
                        gate_top(t - 1)
                    if h == 11:
                        gate_weight(t - 1)
                        combine(t - 1, 0)

            def consume_b(s):
                h, t = s.h, s.t
                if not s.first:
                    if h == 1:
                        take_out(t - 1, s)
                    if h == 2:
                        third_norm(t - 1, 1)
                    if h == 3:
                        third_apply(t - 1)
                    if h == 4:
                        fourth_norm(t - 1, 1)
                    if h == 5:
                        fourth_apply(t - 1)
                    if h == 6:
                        h_lo(t - 1, 1)
                    if h == 7:
                        relu_lo(t - 1, 1)
                    if h == 11:
                        combine(t - 1, 1)
                if not s.last:
                    if h == 0:
                        first_norm(t + 1, 0)
                    if h == 2:
                        p_apply(t + 1, 1)
                    if h == 6:
                        second_norm(t + 1, 0)
                    if h == 7:
                        second_norm(t + 1, 1)

            def step(s):
                if s.h == 14 and not s.last:
                    x_move(s.t + 1, s)
                if s.has(1):
                    sq_lo(s)
                p_hi(s, 0)
                p_hi(s, 1)
                p_lo(s, 0)
                p_lo(s, 1)
                if s.h == 15 and not s.last:
                    k_lo(s.t + 1)
                if s.has(1):
                    q_norms(s)
                    q_lo(s)
                consume_a(s)
                if s.has(-1):
                    o_norm(s)
                consume_b(s)

            dve.memset(eps_ln[:, :], LN_EPS).then_inc(eps_done, 1)
            dve.memset(eps_q[:, :], L2_EPS / (SCALE * SCALE) * ONE).then_inc(eps_done, 1)
            dve.memset(eps_k[:, :], L2_EPS * ONE).then_inc(eps_done, 1)
            dve.memset(fones, ONE).then_inc(ones_done, 1)
            dve.wait_ge(ones_done, 1)
            dve.tensor_copy(ones[:, :], fones).then_inc(ones_done, 1)
            dve.wait_ge(c_exp, 1)
            dve.tensor_scalar(c_e[:, :, :], c_e[:, :, :], 1.0, None, ALU.add).then_inc(c_chain, 1)
            dve.wait_ge(c_chain, 1)
            dve.reciprocal(c_s[:, :, :], c_e[:, :, :]).then_inc(c_chain, 1)
            dve.wait_ge(c_chain, 2)
            dve.tensor_tensor(c_s[:, :, :], c_sb[:, :, :], c_s[:, :, :], ALU.mult).then_inc(c_chain, 1)
            first_norm(0, 0)
            first_norm(0, 1)
            first_newton(0)
            p_apply(0, 0)
            p_apply(0, 1)
            dve.wait_ge(wkv_hi, 1)
            sub(wkv_l[:, :, :], ss[:, :].rearrange("p (c n) -> p c n", c=DC), wkv_h[:, :, :].bitcast(F32)).then_inc(wkv_lo, 1)
            banks = (ps_sim[0:B, 0, :], ps_sim[0:B, 1, :], ps_o[0:B, :])
            m = mod_a[0:B, :, :, :].rearrange("b e k d -> b (e k) d")
            dve.wait_ge(mod_mm, 3)
            dve.wait_ge(gout_in, 16)
            n_fix = 0

            def row(k):
                return mod_rows[k // 4][:, k % 4, :]

            def fix(ins):
                nonlocal n_fix
                n_fix += 1
                ins.then_inc(mod_fix, 1)
                dve.wait_ge(mod_fix, n_fix)

            fix(dve.tensor_copy(row(0), banks[0][:, 0:D]))
            fix(dve.tensor_scalar(row(1), banks[0][:, D:2 * D], 1.0, None, ALU.add))
            for k, src in ((2, banks[1][:, 0:D]), (5, banks[2][:, D:2 * D])):
                fix(dve.tensor_scalar(m[:, 0, :], src, 0.0, 2.0, ALU.is_ge, ALU.mult))
                fix(dve.scalar_tensor_tensor(m[:, 1, :], m[:, 0, :], -1.0, src, ALU.add, ALU.mult))
                fix(dve.tensor_scalar(m[:, 1, :], m[:, 1, :], 0.25, None, ALU.max))
                fix(dve.scalar_tensor_tensor(row(k), m[:, 0, :], -1.0, m[:, 1, :], ALU.add, ALU.mult))
            fix(dve.tensor_tensor(row(2), row(2), gout16, ALU.mult))
            fix(dve.tensor_copy(row(3), banks[1][:, D:2 * D]))
            fix(dve.tensor_scalar(row(4), banks[2][:, 0:D], 1.0, None, ALU.add))
            assert n_fix == MOD_FIX
            for i in range(2):
                dve.wait_ge(w_hi, i + 1)
                sub(wq_l[:, i, :], late[:, i, :], wq_h[:, i, :].bitcast(F32)).then_inc(w_lo, 1)
            second_norm(0, 0)
            second_norm(0, 1)
            second_newton(0)
            p_apply(0, 0)
            p_apply(0, 1)
            dve.wait_ge(gn_in, 16)
            xn_lo(0, 0)
            xn_lo(0, 1)
            x_move(0, None)
            k_norms(0)
            k_lo(0)
            v_lo(0)
            sq_lo(START[1])
            q_norms(START[1])
            q_lo(START[1])
            for i in range(2):
                dve.wait_ge(w_hi, i + 3)
                sub(wo_l[:, 8 * i:8 * (i + 1), :], late[:, i, :].rearrange("p (h n) -> p h n", n=D),
                    wo_h[:, 8 * i:8 * (i + 1), :].bitcast(F32)).then_inc(w_lo, 1)
            run(dve, step)
            o_norm(END[0])
            w = PAIRS - 1
            take_out(w, END[1])
            third_norm(w, 0)
            third_norm(w, 1)
            third_newton(w)
            third_apply(w)
            fourth_norm(w, 0)
            fourth_norm(w, 1)
            fourth_newton(w)
            fourth_apply(w)
            for c in range(DC):
                h_lo(w, c)
            for m_ in range(DC):
                relu_lo(w, m_)
            gate_top(w)
            gate_weight(w)
            combine(w, 0)
            combine(w, 1)

        @block.gpsimd
        def _(pool):
            def tt(o, a, b, op):
                return pool.tensor_tensor(o, a, b, op)

            def rows(m):
                return m.unsqueeze(1).to_broadcast([P, KT, D])

            def p_sum(s):
                pool.wait_ge(exp_done, s.n(0, KT))
                after(pool, ssl_done, s.n(-1))
                tt(ss[:, :], pr[:, 0, :], pr[:, 1, :], ALU.add).then_inc(ss_done, 1)

            def ss_lo(s):
                pool.wait_ge(ssh_done, s.n(0))
                tt(ss_l[:, :], ss[:, :], ss_h[:, :].bitcast(F32), ALU.subtract).then_inc(ssl_done, 1)

            def o_lo(s):
                pool.wait_ge(oh_done, s.n(-2))
                tt(o_l[:, :], on, o_h[:, :].bitcast(F32), ALU.subtract).then_inc(ol_done, 1)

            def modulate_in(u, b):
                pool.wait_ge(p_ln, u * P_LN + (P_LN1 - TILES + (b + 1) * KT))
                pool.wait_ge(moda_in, u * 16 + 16)
                tt(xin[:, b, :, :], xin[:, b, :, :], rows(mod_a[:, b, 1, :]), ALU.mult).then_inc(p_mod, 1)
                pool.wait_ge(p_mod, u * P_MOD + (2 * b + 1))
                tt(xin[:, b, :, :], xin[:, b, :, :], rows(mod_a[:, b, 0, :]), ALU.add).then_inc(p_mod, 1)

            def ksq_lo(u):
                pool.wait_ge(ksqh_done, u + 1)
                tt(ksq_l[:, :], ksq, ksq_h[:, :].bitcast(F32), ALU.subtract).then_inc(ksql_done, 1)

            def residual(w):
                pool.wait_ge(e_ln, w * E_LN + E_READY)
                pool.wait_ge(modb_in, w * 16 + 16)
                pool.wait_ge(xres_in, w * 16 + 16)
                tt(ox[:, 1, :, :], ox[:, 1, :, :], rows(mod_b[:, 1, 0, :]), ALU.mult).then_inc(e_mod, 1)
                pool.wait_ge(e_mod, w * E_MOD + 1)
                tt(xres[:, 1, :, :], xres[:, 1, :, :], ox[:, 1, :, :], ALU.add).then_inc(e_mod, 1)

            def modulate_mlp(w):
                pool.wait_ge(e_ln, w * E_LN + E_LN1 + E_READY)
                tt(ox[:, 1, :, :], ox[:, 1, :, :], rows(mod_b[:, 1, 2, :]), ALU.mult).then_inc(e_mod, 1)
                pool.wait_ge(e_mod, w * E_MOD + 3)
                tt(ox[:, 1, :, :], ox[:, 1, :, :], rows(mod_b[:, 1, 1, :]), ALU.add).then_inc(e_mod, 1)

            def finish(w, b):
                pool.wait_ge(f_done, w * TILES + (b + 1) * KT)
                tt(ox[:, b, :, :], ox[:, b, :, :], rows(mod_b[:, b, 3, :]), ALU.mult).then_inc(e_mod, 1)
                pool.wait_ge(e_mod, w * E_MOD + (4 + 2 * b + 1))
                tt(ox[:, b, :, :], ox[:, b, :, :], xres[:, b, :, :], ALU.add).then_inc(e_mod, 1)

            def step(s):
                h, t = s.h, s.t
                if s.has(-2):
                    o_lo(s)
                p_sum(s)
                if not s.last and h == 13:
                    ksq_lo(t + 1)
                ss_lo(s)
                if not s.last:
                    if h == 2:
                        modulate_in(t + 1, 0)
                    if h == 4:
                        modulate_in(t + 1, 1)
                if not s.first:
                    if h == 3:
                        residual(t - 1)
                    if h == 5:
                        modulate_mlp(t - 1)
                    if h == 12:
                        finish(t - 1, 0)
                    if h == 13:
                        finish(t - 1, 1)

            pool.memset(ident[:, :], 0.0).then_inc(const_zero, 1)
            pool.wait_ge(const_zero, 1)
            pool.affine_select(out=ident[:, :], in_=ident[:, :], compare_op=ALU.not_equal, fill=1.0, base=0,
                               pattern=[[-1, P]], channel_multiplier=1).then_inc(const_done, 1)
            pool.wait_ge(mod_fix, MOD_FIX)
            pool.dma_start(scratch[:, 0:4, :], mod_rows[0]).then_inc(mod_stored, 16)
            pool.dma_start(scratch[:, 4:6, :], mod_rows[1]).then_inc(mod_stored, 16)
            modulate_in(0, 0)
            modulate_in(0, 1)
            ksq_lo(0)
            def split2(i):
                stage2 = ex[:, :, :].rearrange("p j n -> p (j n)")
                hi, lo, n = ((weg_h, weg_l, EG), (wup_h, wup_l, D), (wdn_h, wdn_l, D))[i]
                src = stage2[:, 0:DC * n].rearrange("p (c n) -> p c n", c=DC)
                pool.wait_ge(w2_in, 32 + 16 * i)
                pool.tensor_copy(hi[:, :, :], src).then_inc(w2_hi, 1)
                pool.wait_ge(w2_hi, i + 1)
                tt(lo[:, :, :], src, hi[:, :, :].bitcast(F32), ALU.subtract).then_inc(w2_lo, 1)

            for i in range(3):
                split2(i)
            run(pool, step)
            o_lo(END[0])
            o_lo(END[1])
            w = PAIRS - 1
            residual(w)
            modulate_mlp(w)
            finish(w, 0)
            finish(w, 1)


def kernel(L0_attn_x, L0_attn_g_norm, L0_attn_Wq, L0_attn_Wkv, L0_attn_Wout, L0_attn_g_out, L0_ffn_W_up,
           L0_ffn_W_down, L0_ffn_W_gate, L0_ffn_W_expert, L0_c, L0_wmod):
    import numpy as np
    import concourse.bacc as bacc
    from concourse.bass_utils import run_bass_kernel_spmd

    nc = bacc.Bacc("TRN2", target_bir_lowering=False, num_devices=1)
    arrays = {
        "x": L0_attn_x, "g_norm_pc": np.transpose(np.reshape(L0_attn_g_norm, (DC, P))), "wq": L0_attn_Wq, "wkv": L0_attn_Wkv, "wo": L0_attn_Wout,
        "g_out": L0_attn_g_out, "wup_t": np.transpose(L0_ffn_W_up), "wdown_t": np.transpose(L0_ffn_W_down),
        "wgate_t": np.transpose(L0_ffn_W_gate), "wexp": L0_ffn_W_expert, "c_t": np.transpose(L0_c), "wmod": L0_wmod,
    }
    arrays = {name: np.ascontiguousarray(a) for name, a in arrays.items()}
    args = [nc.dram_tensor(name, a.shape, mybir.dt.from_np(a.dtype), kind="ExternalInput").ap()
            for name, a in arrays.items()]
    scratch = nc.dram_tensor("modulation", (B, 6, D), F32, kind="Internal").ap()
    out = nc.dram_tensor("out", (B, N, D), F32, kind="ExternalOutput").ap()
    adaln_block(nc, *args, scratch, out)
    r = run_bass_kernel_spmd(nc, [arrays], core_ids=[0])
    return r.results[0]["out"]
```

```python
from contextlib import ExitStack

import concourse.bass as bass
from concourse import mybir

F32 = mybir.dt.float32
F32R = mybir.dt.float32r
ALU = mybir.AluOpType
ACT = mybir.ActivationFunctionType


B, N, D = 16, 256, 256
HEADS, DH = 16, 128
P = 128
DC = D // P
PAIRS = B // 2
TOK = 2 * N
KT = N // P
TILES = TOK // P
EXPERTS = 8
EG = D + EXPERTS
LN_EPS = 1e-5
SCALE = 16.0
L2_EPS = 1e-12
ONE = 1.0 / SCALE
NEWTON = 4
P_LN1 = 3 * TILES + NEWTON
P_LN = 2 * P_LN1
P_MOD = 4
E_READY = 2 * TILES + NEWTON + KT
E_LN1 = E_READY + 2 * KT
E_LN = 2 * E_LN1
E_MOD = 8
MOD_FIX = 13
GATE = 4 + 5


def adaln_block(nc, x, g_norm_pc, wq, wkv, wo, g_out, wup_t, wdown_t, wgate_t, wexp, c_t, wmod, scratch, out):
    x_v = x.rearrange("(u b) (j p) d -> u p b j d", b=2, p=P)
    out_v = out.rearrange("(u b) (j p) d -> u p b j d", b=2, p=P)
    mod_v = scratch.rearrange("(u b) k d -> u b k d", b=2)

    with ExitStack() as ctx:
        def sb(name, shape, dt=F32):
            return ctx.enter_context(nc.sbuf_tensor(name, shape, dt))

        def psum(name, shape):
            return ctx.enter_context(nc.psum_tensor(name, shape, F32))

        def sem(name):
            return ctx.enter_context(nc.semaphore(name))

        ps_q = psum("ps_q", [P, TOK])
        ps_s = psum("ps_s", [P, TOK])
        ps_sim = psum("ps_sim", [P, KT, TOK])
        ps_o = psum("ps_o", [P, TOK])
        ps_out = psum("ps_out", [P, TILES, D])
        ps_x = psum("ps_x", [P, TOK])

        wq_h, wq_l = sb("wq_h", [P, DC, HEADS * DH], F32R), sb("wq_l", [P, DC, HEADS * DH], F32R)
        wo_h, wo_l = sb("wo_h", [P, HEADS, D], F32R), sb("wo_l", [P, HEADS, D], F32R)
        wkv_h, wkv_l = sb("wkv_h", [P, DC, 2 * DH], F32R), sb("wkv_l", [P, DC, 2 * DH], F32R)
        wup_h, wup_l = sb("wup_h", [P, DC, D], F32R), sb("wup_l", [P, DC, D], F32R)
        wdn_h, wdn_l = sb("wdn_h", [P, DC, D], F32R), sb("wdn_l", [P, DC, D], F32R)
        weg_h, weg_l = sb("weg_h", [P, DC, EG], F32R), sb("weg_l", [P, DC, EG], F32R)
        ones = sb("ones", [P, P], F32R)
        ident = sb("ident", [P, P])
        gn = sb("gn", [P, DC])

        xn_h, xn_l = sb("xn_h", [P, DC, TOK], F32R), sb("xn_l", [P, DC, TOK], F32R)
        xc_h, xc_l = sb("xc_h", [P, DC, TOK], F32R), sb("xc_l", [P, DC, TOK], F32R)
        k_h, k_l = sb("k_h", [P, TOK], F32R), sb("k_l", [P, TOK], F32R)
        v_h, v_l = sb("v_h", [P, TILES, DH], F32R), sb("v_l", [P, TILES, DH], F32R)
        xin = sb("xin", [P, 2, KT, D])
        xin_flat = xin[:, :, :, :].rearrange("p b j d -> p (b j d)")
        ksq, kn = xin_flat[:, 0:TOK], xin_flat[:, TOK:2 * TOK]
        kr, vt = ksq, ksq
        ksq_h, ksq_l = sb("ksq_h", [P, TOK], F32R), sb("ksq_l", [P, TOK], F32R)
        mod_a = sb("mod_a", [P, 2, 2, D])
        late = sb("late", [P, 2, 2048])
        mod_b = late[:, 0, :].rearrange("p (b k d) -> p b k d", b=2, k=4)
        xres = late[:, 1, 0:1024].rearrange("p (b j d) -> p b j d", b=2, j=KT)
        ox = late[:, 1, 1024:2048].rearrange("p (b j d) -> p b j d", b=2, j=KT)
        ht_h, ht_l = sb("ht_h", [P, DC, TOK], F32R), sb("ht_l", [P, DC, TOK], F32R)
        rt_h, rt_l = sb("rt_h", [P, DC, TOK], F32R), sb("rt_l", [P, DC, TOK], F32R)
        ex = sb("ex", [P, TILES, EG])

        sq = sb("sq", [P, TOK])
        sq_h, sq_l = sb("sq_h", [P, TOK], F32R), sb("sq_l", [P, TOK], F32R)
        fones = sq[:, TOK - P:TOK]
        q_work = sb("q_work", [P, 2, TOK])
        rq, qn = q_work[:, 0, :], q_work[:, 1, :]
        q_h, q_l = sb("q_h", [P, TOK], F32R), sb("q_l", [P, TOK], F32R)
        pr = sb("pr", [P, KT, TOK])
        pr_h, pr_l = sb("pr_h", [P, 2, KT, TOK], F32R), sb("pr_l", [P, 2, KT, TOK], F32R)
        ss = sb("ss", [P, TOK])
        ss_h, ss_l = sb("ss_h", [P, TOK], F32R), sb("ss_l", [P, TOK], F32R)
        o_work = sb("o_work", [P, 2, TOK])
        rden, on = o_work[:, 0, :], o_work[:, 1, :]
        o_h, o_l = sb("o_h", [P, TOK], F32R), sb("o_l", [P, TOK], F32R)

        ln_p = (sb("st_p", [P, TILES, 6]), sb("mv_p", [P, TILES, 2]), sb("y0_p", [P, TILES]), sb("nf_p", [P, TILES]), sb("rs_p", [P, TILES]))
        ln_e = (sb("st_e", [P, TILES, 6]), sb("mv_e", [P, TILES, 2]), sb("y0_e", [P, TILES]), sb("nf_e", [P, TILES]), sb("rs_e", [P, TILES]))
        eps_ln, eps_q, eps_k = sb("eps_ln", [P, 1]), sb("eps_q", [P, 1]), sb("eps_k", [P, 1])
        top = sb("top", [P, TILES, 8])
        g_d, g_e, g_r = sb("g_d", [P, TILES, 2]), sb("g_e", [P, TILES, 2]), sb("g_r", [P, TILES, 2])
        g_s, g_i, g_w = sb("g_s", [P, TILES]), sb("g_i", [P, TILES]), sb("g_w", [P, TILES])
        c_sb, c_e, c_s = sb("c_sb", [P, DC, B]), sb("c_e", [P, DC, B]), sb("c_s", [P, DC, B])
        gout16 = sq[0:B, 0:D]
        mod_rows = (pr[0:B, :, :].rearrange("b c (k d) -> b (c k) d", d=D),
                    q_work[0:B, 0, :].rearrange("b (k d) -> b k d", d=D))

        c_in, gn_in, gout_in = sem("c_in"), sem("gn_in"), sem("gout_in")
        wmod_in = [sem(f"wmod_in{n}") for n in range(3)]
        wkv_in, w2_in = sem("wkv_in"), sem("w2_in")
        stage_in = [sem("stage_in0"), sem("stage_in1")]
        xin_in, moda_in, xres_in, modb_in = sem("xin_in"), sem("moda_in"), sem("xres_in"), sem("modb_in")
        out_stored, moda_stored, modb_stored = sem("out_stored"), sem("moda_stored"), sem("modb_stored")
        const_zero, const_done, ones_done, eps_done = sem("const_zero"), sem("const_done"), sem("ones_done"), sem("eps_done")
        w_hi, w_lo = sem("w_hi"), sem("w_lo")
        wkv_hi, wkv_lo = sem("wkv_hi"), sem("wkv_lo")
        w2_hi, w2_lo = sem("w2_hi"), sem("w2_lo")
        c_exp, c_chain, mod_mm, mod_fix = sem("c_exp"), sem("c_chain"), sem("mod_mm"), sem("mod_fix")
        p_ln, p_mod, p_rs = sem("p_ln"), sem("p_mod"), sem("p_rs")
        xt_tr, xnh_done, xnl_done = sem("xt_tr"), sem("xnh_done"), sem("xnl_done")
        xch_done, xcl_done = sem("xch_done"), sem("xcl_done")
        kproj_done, ksq_done, ksqh_done, ksql_done = sem("kproj_done"), sem("ksq_done"), sem("ksqh_done"), sem("ksql_done")
        ksum_done, kln_done, rk_done, kn_done, kh_done, kl_done = sem("ksum_done"), sem("kln_done"), sem("rk_done"), sem("kn_done"), sem("kh_done"), sem("kl_done")
        vproj_done, vt_done, vtr_done, vh_done, vl_done = sem("vproj_done"), sem("vt_done"), sem("vtr_done"), sem("vh_done"), sem("vl_done")
        qproj_done, sq_done, sqh_done, sql_done = sem("qproj_done"), sem("sq_done"), sem("sqh_done"), sem("sql_done")
        qsum_done, qln_done, rq_done, qn_done, qh_done, ql_done = sem("qsum_done"), sem("qln_done"), sem("rq_done"), sem("qn_done"), sem("qh_done"), sem("ql_done")
        sim_done, exp_done, ph_done, pl_done = sem("sim_done"), sem("exp_done"), sem("ph_done"), sem("pl_done")
        ss_done, ssh_done, ssl_done, den_done = sem("ss_done"), sem("ssh_done"), sem("ssl_done"), sem("den_done")
        av_done, dln_done, rden_done, on_done, oh_done, ol_done = sem("av_done"), sem("dln_done"), sem("rden_done"), sem("on_done"), sem("oh_done"), sem("ol_done")
        out_done = sem("out_done")
        oxa_done, oxd_done, e_ln, e_mod, e_rs = sem("oxa_done"), sem("oxd_done"), sem("e_ln"), sem("e_mod"), sem("e_rs")
        h_tr, hh_done, hl_done = sem("h_tr"), sem("hh_done"), sem("hl_done")
        up_done, rh_done, rl_done = sem("up_done"), sem("rh_done"), sem("rl_done")
        xg_done, ex_done, gate, gate_exp = sem("xg_done"), sem("ex_done"), sem("gate"), sem("gate_exp")
        shared_done, f_done, tail_done = sem("shared_done"), sem("f_done"), sem("tail_done")
        start_mod = sem("start_mod")

        def after(eng, s, value):
            if isinstance(value, int) and value <= 0:
                return
            eng.wait_ge(s, value)

        class Step:

            def __init__(self, t, t16, h, first, last, past=False):
                self.t, self.t16, self.h, self.first, self.last, self.past = t, t16, h, first, last, past

            def n(self, d, per=1, k=None):
                k = per if k is None else k
                base = self.t16 if per == 1 else self.t * (HEADS * per)
                return base + (per * (self.h + d) + k)

            def has(self, d):
                if self.past:
                    return d < 0
                return not (self.first and self.h + d < 0) and not (self.last and self.h + d >= HEADS)

        def run(eng, step):
            for h in range(HEADS):
                step(Step(0, 0, h, True, False))
            with eng.Fori(1, PAIRS - 1) as t:
                t16 = t * HEADS
                for h in range(HEADS):
                    step(Step(t, t16, h, False, False))
            for h in range(HEADS):
                step(Step(PAIRS - 1, (PAIRS - 1) * HEADS, h, False, True))

        END = [Step(PAIRS, PAIRS * HEADS, h, False, True, past=True) for h in range(2)]
        START = [Step(0, 0, h, False, False) for h in (-2, -1)]

        def start(u):
            return isinstance(u, int) and u == 0

        def final(w):
            return isinstance(w, int) and w == PAIRS - 1

        def xt_bank(u, c):
            return ps_q[:, :] if start(u) and c == 1 else ps_x[:, :]

        def v_bank(u):
            return ps_out[:, 0:KT, :].rearrange("p j d -> p (j d)") if start(u) else ps_x[:, :]

        def vtr_bank(u):
            return ps_out[:, KT:TILES, :].rearrange("p j d -> p (j d)") if start(u) else ps_x[:, :]

        def vt_place(u):
            return on if start(u) else vt

        def ht_bank(w, c):
            return (ps_q, ps_s)[c][:, :] if final(w) else ps_x[:, :]

        def pair_bank(w, i):
            return ps_sim[:, i, :] if final(w) else ps_x[:, :]

        def ex_bank(w, j):
            return ((ps_q, ps_s, ps_o, ps_x)[j] if final(w) else ps_x)[:, 0:EG]

        block = ctx.enter_context(nc.Block())

        @block.sync
        def _(sp):
            def load_x(u):
                sp.wait_ge(kl_done, u)
                sp.wait_ge(vtr_done, u)
                sp.dma_start(xin[:, :, :, :], x_v[u]).then_inc(xin_in, 16)
                sp.dma_start(mod_a[:, :, :, :], mod_v[u, :, 0:2, :].partition_broadcast(P)).then_inc(moda_in, 16)

            def load_late(w):
                after(sp, e_mod, w * E_MOD)
                sp.dma_start(mod_b, mod_v[w, :, 2:6, :].partition_broadcast(P)).then_inc(modb_in, 16)
                sp.dma_start(xres, x_v[w]).then_inc(xres_in, 16)

            def store(w):
                sp.wait_ge(e_mod, w * E_MOD + E_MOD)
                sp.dma_start(out_v[w], ox).then_inc(out_stored, 16)

            sp.dma_start(c_sb[:, :, :], c_t.rearrange("(c p) b -> p c b", p=P)).then_inc(c_in, 16)
            sp.dma_start(xin[:, :, :, :], x_v[0]).then_inc(xin_in, 16)
            wmod_v = wmod.rearrange("(c p) n -> p c n", p=P)
            for n, place in enumerate((pr, q_work, o_work)):
                sp.dma_start(place[:, :, :], wmod_v[:, :, n * 512:(n + 1) * 512]).then_inc(wmod_in[n], 16)
            sp.dma_start(gout16, g_out.partition_broadcast(B)).then_inc(gout_in, 16)
            sp.dma_start(gn[:, :], g_norm_pc).then_inc(gn_in, 16)
            sp.dma_start(ss[:, :].rearrange("p (c n) -> p c n", c=DC),
                         wkv.rearrange("(c p) n -> p c n", p=P)).then_inc(wkv_in, 16)
            wq_v = wq.rearrange("(c p) n -> c p n", p=P)
            wo_v = wo.rearrange("(g h p) n -> g p h n", g=2, p=P)
            for i in range(2):
                sp.dma_start(late[:, i, :], wq_v[i]).then_inc(stage_in[i], 16)
            stage2 = ex[:, :, :].rearrange("p j n -> p (j n)")

            def load_w2(i, w):
                after(sp, w2_lo, i)
                if i == 0:
                    place = stage2[:, 0:DC * EG].rearrange("p (c n) -> p c n", c=DC)
                    sp.dma_start(place[:, :, 0:D], w.rearrange("(c p) n -> p c n", p=P)).then_inc(w2_in, 16)
                    sp.dma_start(place[:, :, D:EG], wgate_t.rearrange("(c p) n -> p c n", p=P)).then_inc(w2_in, 16)
                else:
                    sp.dma_start(stage2[:, 0:DC * D].rearrange("p (c n) -> p c n", c=DC),
                                 w.rearrange("(c p) n -> p c n", p=P)).then_inc(w2_in, 16)

            def load_wo(i):
                sp.wait_ge(w_lo, i + 1)
                sp.dma_start(late[:, i, :].rearrange("p (h n) -> p h n", n=D), wo_v[i]).then_inc(stage_in[i], 16)

            load_w2(0, wexp)
            sp.wait_ge(moda_stored, 16)
            sp.dma_start(mod_a[:, :, :, :], mod_v[0, :, 0:2, :].partition_broadcast(P)).then_inc(moda_in, 16)
            load_w2(1, wup_t)
            load_wo(0)
            load_w2(2, wdown_t)
            load_wo(1)
            sp.wait_ge(modb_stored, 32)
            load_x(1)
            sp.wait_ge(w_lo, 4)
            with sp.Fori(1, PAIRS - 1) as t:
                load_late(t - 1)
                load_x(t + 1)
                store(t - 1)
            load_late(PAIRS - 2)
            store(PAIRS - 2)
            w = PAIRS - 1
            load_late(w)
            sp.wait_ge(e_mod, w * E_MOD + 6)
            sp.dma_start(out_v[w][:, 0], ox[:, 0, :, :]).then_inc(out_stored, 16)
            sp.wait_ge(tail_done, 2)
            sp.dma_start(out_v[w][:, 1], ox[:, 1, :, :]).then_inc(out_stored, 16)
            sp.wait_ge(out_stored, 16 * (PAIRS + 1))

        @block.tensor
        def _(pe):
            def mm3(o, wh, wl, mh, ml, start, stop, **kw):
                pe.matmul(o, wh, mh, start=start, stop=False, **kw)
                pe.matmul(o, wh, ml, start=False, stop=False, **kw)
                return pe.matmul(o, wl, mh, start=False, stop=stop, **kw)

            def project(o, wh, wl, cols, xh, xl):
                for c in range(DC):
                    last = mm3(o, wh[:, c, cols], wl[:, c, cols], xh[:, c, :], xl[:, c, :], c == 0, c == DC - 1)
                return last

            def column_sums(hi, lo):
                pe.matmul(ps_s[:, :], ones[:, :], hi, start=True, stop=False)
                return pe.matmul(ps_s[:, :], ones[:, :], lo, start=False, stop=True)

            def scores(s):
                pe.wait_ge(ql_done, s.n(0))
                if s.h == 0:
                    pe.wait_ge(kl_done, s.t + 1)
                for c in range(KT):
                    after(pe, exp_done, s.n(-1, KT, c + 1))
                    for b in range(2):
                        kt = slice((b * KT + c) * P, (b * KT + c + 1) * P)
                        tok = slice(b * N, (b + 1) * N)
                        last = mm3(ps_sim[:, c, tok], k_h[:, kt], k_l[:, kt], q_h[:, tok], q_l[:, tok], True, True)
                    last.then_inc(sim_done, 1)

            def q_norm(s):
                pe.wait_ge(sql_done, s.n(1))
                after(pe, dln_done, s.n(-2))
                if s.h == HEADS - 1 and not s.last:
                    pe.wait_ge(kln_done, s.t + 2)
                column_sums(sq_h[:, :], sq_l[:, :]).then_inc(qsum_done, 1)

            def attend(s, b):
                if b == 0:
                    pe.wait_ge(pl_done, s.n(-1, KT))
                    after(pe, on_done, s.n(-2))
                    if s.h == 1:
                        pe.wait_ge(vl_done, s.t + 1)
                par = (s.h - 1) % 2
                tok = slice(b * N, (b + 1) * N)
                for c in range(KT):
                    i = b * KT + c
                    last = mm3(ps_o[:, tok], v_h[:, i, :], v_l[:, i, :], pr_h[:, par, c, tok], pr_l[:, par, c, tok],
                               c == 0, c == KT - 1)
                if b == 1:
                    last.then_inc(av_done, 1)

            def softmax_sums(s):
                pe.wait_ge(ssl_done, s.n(-1))
                if s.has(1):
                    pe.wait_ge(qln_done, s.n(1))
                column_sums(ss_h[:, :], ss_l[:, :]).then_inc(den_done, 1)

            def q_project(s):
                after(pe, qn_done, s.n(1))
                if s.h + 2 == HEADS:
                    pe.wait_ge(xnl_done, (s.t + 2) * DC)
                if s.h == 0:
                    pe.wait_ge(xch_done, s.t + 1)
                    pe.wait_ge(xcl_done, s.t + 1)
                h = (s.h + 2) % HEADS
                src = (xn_h, xn_l) if h < 2 else (xc_h, xc_l)
                project(ps_q[:, :], wq_h, wq_l, slice(h * DH, (h + 1) * DH), *src).then_inc(qproj_done, 1)

            def out_project(s, b):
                if b == 0:
                    pe.wait_ge(ol_done, s.n(-2))
                if s.h == 2 and b == 0:
                    after(pe, oxa_done, s.t)
                    after(pe, oxd_done, s.t)
                    if s.first:
                        pe.wait_ge(w_lo, 4)
                h = (s.h - 2) % HEADS
                for j in range(b * KT, (b + 1) * KT):
                    tile = slice(j * P, (j + 1) * P)
                    last = mm3(ps_out[:, j, :], o_h[:, tile], o_l[:, tile], wo_h[:, h, :], wo_l[:, h, :],
                               h == 0 and j % 2 == 0, h == HEADS - 1, skip_group_check=True)
                if b == 1:
                    last.then_inc(out_done, 1)

            def x_transpose(u, c, first):
                if c == 0:
                    pe.wait_ge(p_ln, u * P_LN + P_LN)
                if not start(u):
                    if first:
                        pe.wait_ge(xnl_done, u * DC + c) if c else pe.wait_ge(vl_done, u)
                    else:
                        pe.wait_ge(f_done, (u - 1) * TILES) if c else pe.wait_ge(ex_done, (u - 1) * TILES)
                for i in range(TILES):
                    last = pe.transpose(xt_bank(u, c)[:, i * P:(i + 1) * P], xin[:, i // KT, i % KT, c * P:(c + 1) * P],
                                        ident[:, :])
                last.then_inc(xt_tr, 1)

            def k_project(u):
                pe.wait_ge(xnl_done, u * DC + DC)
                project(ps_x[:, :], wkv_h, wkv_l, slice(0, DH), xn_h, xn_l).then_inc(kproj_done, 1)

            def k_norm(u, s):
                pe.wait_ge(ksql_done, u + 1)
                if s is not None:
                    after(pe, dln_done, s.n(-1))
                column_sums(ksq_h[:, :], ksq_l[:, :]).then_inc(ksum_done, 1)

            def v_project(u):
                if not start(u):
                    pe.wait_ge(kn_done, u + 1)
                project(v_bank(u), wkv_h, wkv_l, slice(DH, 2 * DH), xn_h, xn_l).then_inc(vproj_done, 1)

            def v_transpose(u):
                pe.wait_ge(vt_done, u + 1)
                for i in range(TILES):
                    last = pe.transpose(vtr_bank(u)[:, i * P:(i + 1) * P], vt_place(u)[:, i * P:(i + 1) * P], ident[:, :])
                last.then_inc(vtr_done, 1)

            def h_transpose(w, c):
                if c == 0:
                    pe.wait_ge(e_ln, w * E_LN + E_LN)
                    pe.wait_ge(e_mod, w * E_MOD + 4)
                    if not final(w):
                        pe.wait_ge(vl_done, w + 2)
                elif not final(w):
                    pe.wait_ge(hl_done, w * DC + c)
                for i in range(TILES):
                    last = pe.transpose(ht_bank(w, c)[:, i * P:(i + 1) * P], ox[:, i // KT, i % KT, c * P:(c + 1) * P],
                                        ident[:, :])
                last.then_inc(h_tr, 1)

            def up(w, m):
                if m == 0:
                    pe.wait_ge(hl_done, w * DC + DC)
                elif not final(w):
                    pe.wait_ge(rl_done, w * DC + m)
                project(pair_bank(w, m), wup_h, wup_l, slice(m * P, (m + 1) * P), ht_h, ht_l).then_inc(up_done, 1)

            def expert(w, j):
                if not final(w):
                    if j == 0:
                        pe.wait_ge(rl_done, w * DC + DC)
                    else:
                        pe.wait_ge(ex_done, w * TILES + j)
                elif j == TILES - 1:
                    pe.wait_ge(f_done, w * TILES)
                tile = slice(j * P, (j + 1) * P)
                for c in range(DC):
                    last = mm3(ex_bank(w, j), ht_h[:, c, tile], ht_l[:, c, tile], weg_h[:, c, :], weg_l[:, c, :],
                               c == 0, c == DC - 1)
                last.then_inc(xg_done, 1)

            def shared(w, b, last_pair):
                if final(w):
                    pe.wait_ge(rl_done, w * DC + DC)
                elif b == 0 and last_pair:
                    pe.wait_ge(ex_done, w * TILES + TILES)
                elif b == 0:
                    pe.wait_ge(xnl_done, (w + 2) * DC + 1)
                else:
                    pe.wait_ge(f_done, w * TILES + KT)
                for j in range(KT):
                    tile = slice((b * KT + j) * P, (b * KT + j + 1) * P)
                    for c in range(DC):
                        last = mm3(pair_bank(w, b)[:, j * D:(j + 1) * D], rt_h[:, c, tile], rt_l[:, c, tile],
                                   wdn_h[:, c, :], wdn_l[:, c, :], c == 0, c == DC - 1)
                last.then_inc(shared_done, 1)

            def piece_a(s):
                h, t = s.h, s.t
                if not s.first:
                    if h == 8:
                        h_transpose(t - 1, 0)
                    if h == 9:
                        up(t - 1, 0)
                    if h == 10:
                        expert(t - 1, 0)
                    if h == 11:
                        expert(t - 1, 2)
                    if h == 13:
                        shared(t - 1, 1, s.last)
                if not s.last:
                    if h == 12:
                        x_transpose(t + 1, 0, s.first)
                    if h == 14:
                        k_project(t + 1)
                    if h == 15:
                        v_project(t + 1)

            def piece_b(s):
                h, t = s.h, s.t
                if not s.first:
                    if h == 8:
                        h_transpose(t - 1, 1)
                    if h == 9:
                        up(t - 1, 1)
                    if h == 10:
                        expert(t - 1, 1)
                    if h == 11:
                        expert(t - 1, 3)
                    if h == 12:
                        shared(t - 1, 0, s.last)
                if not s.last:
                    if h == 13:
                        x_transpose(t + 1, 1, s.first)
                    if h == 14:
                        k_norm(t + 1, s)
                    if h == 15:
                        v_transpose(t + 1)

            def step(s):
                scores(s)
                if s.has(-1):
                    attend(s, 0)
                if s.has(1):
                    q_norm(s)
                if s.has(-1):
                    attend(s, 1)
                piece_a(s)
                if s.has(-2):
                    out_project(s, 0)
                if s.has(-1):
                    softmax_sums(s)
                if s.has(-2):
                    out_project(s, 1)
                if s.has(2):
                    q_project(s)
                piece_b(s)

            pe.wait_ge(c_chain, 3)
            for n, (place, bank) in enumerate(((pr, ps_sim[:, 0, :]), (q_work, ps_sim[:, 1, :]), (o_work, ps_o[:, :]))):
                pe.wait_ge(wmod_in[n], 16)
                for c in range(DC):
                    last = pe.matmul(bank[0:B, :], c_s[:, c, :], place[:, c, :], start=(c == 0), stop=(c == DC - 1))
                last.then_inc(mod_mm, 1)
            pe.wait_ge(const_done, 1)
            for c in range(DC):
                x_transpose(0, c, True)
            pe.wait_ge(wkv_lo, 1)
            k_project(0)
            pe.wait_ge(mod_fix, MOD_FIX)
            v_project(0)
            pe.wait_ge(ones_done, 2)
            pe.wait_ge(w_lo, 2)
            q_project(START[0])
            k_norm(0, None)
            v_transpose(0)
            pe.wait_ge(kln_done, 1)
            q_norm(START[1])
            q_project(START[1])
            run(pe, step)
            attend(END[0], 0)
            attend(END[0], 1)
            softmax_sums(END[0])
            for step_ in END:
                out_project(step_, 0)
                out_project(step_, 1)
            w = PAIRS - 1
            h_transpose(w, 0)
            h_transpose(w, 1)
            up(w, 0)
            up(w, 1)
            for j in range(TILES):
                expert(w, j)
            shared(w, 0, True)
            shared(w, 1, True)

        @block.scalar
        def _(act):
            def copy(o, i, **kw):
                return act.activation(o, i, ACT.Copy, **kw)

            def exps(s):
                for c in range(KT):
                    act.wait_ge(sim_done, s.n(0, KT, c + 1))
                    after(act, pl_done, s.n(-1, KT, c + 1))
                    if c == 0:
                        after(act, ss_done, s.n(-1))
                    act.activation(pr[:, c, :], ps_sim[:, c, :], ACT.Exp).then_inc(exp_done, 1)

            def den_ln(s):
                act.wait_ge(den_done, s.n(-1))
                after(act, on_done, s.n(-2))
                act.activation(rden, ps_s[:, :], ACT.Ln, scale=1 / ONE).then_inc(dln_done, 1)

            def den_recip(s):
                act.wait_ge(dln_done, s.n(-1))
                act.activation(rden, rden, ACT.Exp, scale=-1.0).then_inc(rden_done, 1)

            def rsqrt(o, i, eps, ln_sem, done_sem, count):
                act.activation(o, i, ACT.Ln, bias=eps[:, :]).then_inc(ln_sem, 1)
                act.wait_ge(ln_sem, count)
                act.activation(o, o, ACT.Exp, scale=-0.5).then_inc(done_sem, 1)

            def q_rsqrt(s):
                act.wait_ge(qsum_done, s.n(1))
                after(act, qn_done, s.n(0))
                rsqrt(rq, ps_s[:, :], eps_q, qln_done, rq_done, s.n(1))

            def ss_hi(s):
                act.wait_ge(ss_done, s.n(0))
                after(act, den_done, s.n(-1))
                copy(ss_h[:, :], ss[:, :]).then_inc(ssh_done, 1)

            def o_hi(s):
                act.wait_ge(on_done, s.n(-2))
                after(act, out_done, s.n(-3))
                copy(o_h[:, :], on).then_inc(oh_done, 1)

            def squares(s):
                act.wait_ge(qproj_done, s.n(1))
                after(act, sql_done, s.n(0))
                act.activation(sq[:, :], ps_q[:, :], ACT.Square).then_inc(sq_done, 1)
                after(act, qsum_done, s.n(0))
                act.activation(sq_h[:, :], ps_q[:, :], ACT.Square).then_inc(sqh_done, 1)

            def xn_hi(u, c):
                act.wait_ge(xt_tr, u * DC + c + 1)
                if c == 0:
                    after(act, vproj_done, u)
                    after(act, xcl_done, u)
                copy(xn_h[:, c, :], xt_bank(u, c), scale=gn[:, c:c + 1]).then_inc(xnh_done, 1)

            def x_move(s):
                act.wait_ge(qproj_done, s.n(1))
                act.wait_ge(xnh_done, s.t * DC + DC)
                copy(xc_h[:, :, :], xn_h[:, :, :].bitcast(F32)).then_inc(xch_done, 1)

            def k_squares(u):
                act.wait_ge(kproj_done, u + 1)
                act.activation(ksq, ps_x[:, :], ACT.Square).then_inc(ksq_done, 1)
                act.activation(ksq_h[:, :], ps_x[:, :], ACT.Square).then_inc(ksqh_done, 1)

            def k_rsqrt(u):
                act.wait_ge(ksum_done, u + 1)
                act.wait_ge(ksql_done, u + 1)
                rsqrt(kr, ps_s[:, :], eps_k, kln_done, rk_done, u + 1)

            def ln_rsqrt(ln, ln_sem, ln_count, ln_chain, count):
                _, mv, y0, _, _ = ln
                act.wait_ge(ln_sem, ln_count)
                act.activation(y0[:, :], mv[:, :, 1], ACT.Ln, bias=eps_ln[:, :]).then_inc(ln_chain, 1)
                act.wait_ge(ln_chain, count + 1)
                act.activation(y0[:, :], y0[:, :], ACT.Exp, scale=-0.5).then_inc(ln_chain, 1)

            def p_rsqrt(u, k):
                ln_rsqrt(ln_p, p_ln, u * P_LN + (k * P_LN1 + 2 * TILES), p_rs, u * 4 + 2 * k)

            def e_rsqrt(w, k):
                ln_rsqrt(ln_e, e_ln, w * E_LN + (k * E_LN1 + 2 * TILES), e_rs, w * 4 + 2 * k)

            def k_hi(u, s):
                act.wait_ge(kn_done, u + 1)
                if s is not None:
                    act.wait_ge(sim_done, s.n(0, KT))
                copy(k_h[:, :], kn).then_inc(kh_done, 1)

            def v_copy(u):
                act.wait_ge(vproj_done, u + 1)
                if not start(u):
                    act.wait_ge(kn_done, u + 1)
                copy(vt_place(u), v_bank(u)).then_inc(vt_done, 1)

            def v_hi(u, s):
                act.wait_ge(vtr_done, u + 1)
                if s is not None:
                    after(act, av_done, s.n(-1))
                copy(v_h[:, :, :].rearrange("p i d -> p (i d)"), vtr_bank(u)).then_inc(vh_done, 1)

            def take_out(w):
                act.wait_ge(out_done, w * HEADS + HEADS)
                after(act, out_stored, w * 16)
                copy(ox[:, 0, :, :], ps_out[:, 0:KT, :]).then_inc(oxa_done, 1)

            def h_hi(w, c):
                act.wait_ge(h_tr, w * DC + c + 1)
                if c == 0:
                    after(act, xg_done, w * TILES)
                copy(ht_h[:, c, :], ht_bank(w, c)).then_inc(hh_done, 1)

            def relu_hi(w, m):
                act.wait_ge(up_done, w * DC + m + 1)
                if m == 0:
                    after(act, shared_done, w * 2)
                act.activation(rt_h[:, m, :], pair_bank(w, m), ACT.Relu).then_inc(rh_done, 1)

            def take_expert(w, j):
                act.wait_ge(xg_done, w * TILES + j + 1)
                if j == 0:
                    after(act, f_done, w * TILES)
                copy(ex[:, j, :], ex_bank(w, j)).then_inc(ex_done, 1)

            def gate_exps(w):
                act.wait_ge(gate, w * GATE + 5)
                act.activation(g_e[:, :, :], g_d[:, :, :], ACT.Exp).then_inc(gate_exp, 1)

            def guesses(s):
                h, t = s.h, s.t
                if not s.last:
                    if h == 3:
                        p_rsqrt(t + 1, 0)
                if not s.first:
                    if h == 6:
                        e_rsqrt(t - 1, 1)
                    if h == 12:
                        gate_exps(t - 1)

            def consume_a(s):
                h, t = s.h, s.t
                if not s.first:
                    if h == 0:
                        v_hi(t, s)
                    if h == 8:
                        h_hi(t - 1, 0)
                    if h == 9:
                        relu_hi(t - 1, 0)
                    if h == 10:
                        take_expert(t - 1, 0)
                    if h == 11:
                        take_expert(t - 1, 2)
                if not s.last:
                    if h == 12:
                        xn_hi(t + 1, 0)
                    if h == 14:
                        k_squares(t + 1)
                    if h == 15:
                        v_copy(t + 1)

            def late_guesses(s):
                if s.h == 3 and not s.first:
                    e_rsqrt(s.t - 1, 0)
                if s.h == 10 and not s.last:
                    p_rsqrt(s.t + 1, 1)

            def consume_b(s):
                h, t = s.h, s.t
                if not s.first:
                    if h == 2:
                        take_out(t - 1)
                    if h == 9:
                        h_hi(t - 1, 1)
                    if h == 10:
                        relu_hi(t - 1, 1)
                    if h == 11:
                        take_expert(t - 1, 1)
                    if h == 12:
                        take_expert(t - 1, 3)
                if not s.last:
                    if h == 14:
                        xn_hi(t + 1, 1)
                    if h == 15:
                        k_rsqrt(t + 1)

            def step(s):
                if s.has(1):
                    squares(s)
                consume_b(s)
                if s.has(-2):
                    o_hi(s)
                exps(s)
                if s.h == 15 and not s.last:
                    k_hi(s.t + 1, s)
                if s.has(1):
                    q_rsqrt(s)
                guesses(s)
                if s.h == 0:
                    x_move(s)
                consume_a(s)
                if s.has(-1):
                    den_ln(s)
                ss_hi(s)
                if s.has(-1):
                    den_recip(s)
                late_guesses(s)

            def wo_hi(i):
                act.wait_ge(stage_in[i], 32)
                copy(wo_h[:, 8 * i:8 * (i + 1), :], late[:, i, :].rearrange("p (h n) -> p h n", n=D)).then_inc(w_hi, 1)

            act.preload_act_table_set("natural_log_exp_and_others")
            act.wait_ge(c_in, 16)
            act.activation(c_e[:, :, :], c_sb[:, :, :], ACT.Exp, scale=-1.0).then_inc(c_exp, 1)
            act.wait_ge(eps_done, 3)
            p_rsqrt(0, 0)
            act.wait_ge(wkv_in, 16)
            copy(wkv_h[:, :, :], ss[:, :].rearrange("p (c n) -> p c n", c=DC)).then_inc(wkv_hi, 1)
            act.wait_ge(stage_in[0], 16)
            copy(wq_h[:, 0, :], late[:, 0, :]).then_inc(w_hi, 1)
            act.wait_ge(stage_in[1], 16)
            copy(wq_h[:, 1, :], late[:, 1, :]).then_inc(w_hi, 1)
            p_rsqrt(0, 1)
            act.wait_ge(gn_in, 16)
            xn_hi(0, 0)
            xn_hi(0, 1)
            k_squares(0)
            v_copy(0)
            act.wait_ge(modb_stored, 32)
            wo_hi(0)
            squares(START[1])
            k_rsqrt(0)
            k_hi(0, None)
            v_hi(0, None)
            q_rsqrt(START[1])
            wo_hi(1)
            run(act, step)
            o_hi(END[0])
            den_ln(END[0])
            den_recip(END[0])
            o_hi(END[1])
            take_out(PAIRS - 1)
            e_rsqrt(PAIRS - 1, 0)
            e_rsqrt(PAIRS - 1, 1)
            for c in range(DC):
                h_hi(PAIRS - 1, c)
            for m in range(DC):
                relu_hi(PAIRS - 1, m)
            for j in range(TILES):
                take_expert(PAIRS - 1, j)
            gate_exps(PAIRS - 1)

        @block.vector
        def _(dve):
            def sub(o, a, b):
                return dve.tensor_tensor(o, a, b, ALU.subtract)

            def ln_stats(src, i, ln, s):
                dve.bn_stats(ln[0][:, i, :], src[:, i // KT, i % KT, :]).then_inc(s, 1)

            def ln_means(ln, s, base):
                st, mv, _, nf, _ = ln
                dve.wait_ge(s, base + TILES)
                dve.memset(nf[:, :], 0.0)
                for i in range(TILES):
                    dve.bn_aggr(mv[:, i, :], st[:, i, :]).then_inc(s, 1)

            def newton(ln, s, k, guess, guess_count):
                _, mv, y0, nf, rs = ln
                dve.wait_ge(guess, guess_count)
                dve.scalar_tensor_tensor(nf[:, :], mv[:, :, 1], LN_EPS, y0[:, :], ALU.add, ALU.mult).then_inc(s, 1)
                dve.wait_ge(s, k + 1)
                dve.tensor_tensor(nf[:, :], nf[:, :], y0[:, :], ALU.mult).then_inc(s, 1)
                dve.wait_ge(s, k + 2)
                dve.tensor_scalar(nf[:, :], nf[:, :], -0.5, 1.5, ALU.mult, ALU.add).then_inc(s, 1)
                dve.wait_ge(s, k + 3)
                dve.tensor_tensor(rs[:, :], nf[:, :], y0[:, :], ALU.mult).then_inc(s, 1)
                dve.wait_ge(s, k + 4)

            def normal_tile(dst, src, ln, i):
                return dve.tensor_scalar(dst, src, ln[1][:, i, 0:1], ln[4][:, i:i + 1], ALU.subtract, ALU.mult)

            def scale_tile(dst, src, ln, i, m):
                return dve.scalar_tensor_tensor(dst, src, ln[1][:, i, 0:1], m, ALU.subtract, ALU.mult)

            def shift_tile(dst, src, ln, i, m):
                return dve.scalar_tensor_tensor(dst, src, ln[4][:, i:i + 1], m, ALU.mult, ALU.add)

            def q_norms(s):
                dve.wait_ge(rq_done, s.n(1))
                dve.tensor_tensor(qn, ps_q[:, :], rq, ALU.mult).then_inc(qn_done, 1)
                dve.wait_ge(qn_done, s.n(1))
                after(dve, sim_done, s.n(0, KT))
                dve.tensor_copy(q_h[:, :], qn).then_inc(qh_done, 1)

            def sq_lo(s):
                dve.wait_ge(sqh_done, s.n(1))
                sub(sq_l[:, :], sq[:, :], sq_h[:, :].bitcast(F32)).then_inc(sql_done, 1)

            def q_lo(s):
                dve.wait_ge(qh_done, s.n(1))
                sub(q_l[:, :], qn, q_h[:, :].bitcast(F32)).then_inc(ql_done, 1)

            def p_hi(s, c):
                dve.wait_ge(exp_done, s.n(0, KT, c + 1))
                after(dve, av_done, s.n(-2))
                dve.tensor_copy(pr_h[:, s.h % 2, c, :], pr[:, c, :]).then_inc(ph_done, 1)

            def p_lo(s, c):
                dve.wait_ge(ph_done, s.n(0, KT, c + 1))
                sub(pr_l[:, s.h % 2, c, :], pr[:, c, :], pr_h[:, s.h % 2, c, :].bitcast(F32)).then_inc(pl_done, 1)

            def o_norm(s):
                dve.wait_ge(rden_done, s.n(-1))
                dve.wait_ge(av_done, s.n(-1))
                after(dve, oh_done, s.n(-2))
                after(dve, ol_done, s.n(-2))
                dve.tensor_tensor(on, ps_o[:, :], rden, ALU.mult).then_inc(on_done, 1)

            def first_stats(u, i):
                if i == 0:
                    dve.wait_ge(xin_in, u * 16 + 16)
                ln_stats(xin, i, ln_p, p_ln)

            def first_means(u):
                ln_means(ln_p, p_ln, u * P_LN)

            def first_newton(u):
                newton(ln_p, p_ln, u * P_LN + 2 * TILES, p_rs, u * 4 + 2)

            def p_apply(u, i):
                x_i = xin[:, i // KT, i % KT, :]
                normal_tile(x_i, x_i, ln_p, i).then_inc(p_ln, 1)

            def second_stats(u, i):
                if i % KT == 0 and not (start(u) and i == 0):
                    dve.wait_ge(p_mod, u * P_MOD + 2 * (i // KT) + 2)
                ln_stats(xin, i, ln_p, p_ln)

            def second_means(u):
                ln_means(ln_p, p_ln, u * P_LN + P_LN1)

            def second_newton(u):
                newton(ln_p, p_ln, u * P_LN + P_LN1 + 2 * TILES, p_rs, u * 4 + 4)

            def xn_lo(u, c):
                dve.wait_ge(xnh_done, u * DC + c + 1)
                dve.scalar_tensor_tensor(xn_l[:, c, :], xt_bank(u, c), gn[:, c:c + 1], xn_h[:, c, :].bitcast(F32),
                                         ALU.mult, ALU.subtract).then_inc(xnl_done, 1)

            def x_move(s):
                dve.wait_ge(qproj_done, s.n(1))
                dve.wait_ge(xnl_done, s.t * DC + DC)
                dve.tensor_copy(xc_l[:, :, :], xn_l[:, :, :].bitcast(F32)).then_inc(xcl_done, 1)

            def k_norms(u):
                dve.wait_ge(rk_done, u + 1)
                dve.tensor_tensor(kn, ps_x[:, :], kr, ALU.mult).then_inc(kn_done, 1)

            def k_lo(u):
                dve.wait_ge(kh_done, u + 1)
                sub(k_l[:, :], kn, k_h[:, :].bitcast(F32)).then_inc(kl_done, 1)

            def v_lo(u):
                dve.wait_ge(vh_done, u + 1)
                sub(v_l[:, :, :].rearrange("p i d -> p (i d)"), vtr_bank(u),
                    v_h[:, :, :].rearrange("p i d -> p (i d)").bitcast(F32)).then_inc(vl_done, 1)

            def take_out(w, s):
                dve.wait_ge(out_done, w * HEADS + HEADS)
                after(dve, out_stored, w * 16)
                dve.tensor_copy(ox[:, 1, :, :], ps_out[:, KT:2 * KT, :]).then_inc(oxd_done, 1)

            def third_stats(w, i):
                if i % KT == 0:
                    dve.wait_ge(oxd_done if i else oxa_done, w + 1)
                ln_stats(ox, i, ln_e, e_ln)

            def third_means(w):
                ln_means(ln_e, e_ln, w * E_LN)

            def third_newton(w):
                newton(ln_e, e_ln, w * E_LN + 2 * TILES, e_rs, w * 4 + 2)

            def third_apply(w, j):
                normal_tile(ox[:, 1, j, :], ox[:, 1, j, :], ln_e, KT + j).then_inc(e_ln, 1)

            def third_scale(w, j):
                if j == 0:
                    dve.wait_ge(modb_in, w * 16 + 16)
                    dve.wait_ge(xres_in, w * 16 + 16)
                scale_tile(ox[:, 0, j, :], ox[:, 0, j, :], ln_e, j, mod_b[:, 0, 0, :]).then_inc(e_ln, 1)

            def third_shift(w, j):
                if j == 0:
                    dve.wait_ge(e_ln, w * E_LN + E_READY + KT)
                shift_tile(xres[:, 0, j, :], ox[:, 0, j, :], ln_e, j, xres[:, 0, j, :]).then_inc(e_ln, 1)

            def fourth_stats(w, i):
                if i == 0:
                    dve.wait_ge(e_ln, w * E_LN + E_LN1)
                if i == KT:
                    dve.wait_ge(e_mod, w * E_MOD + 2)
                ln_stats(xres, i, ln_e, e_ln)

            def fourth_means(w):
                ln_means(ln_e, e_ln, w * E_LN + E_LN1)

            def fourth_newton(w):
                newton(ln_e, e_ln, w * E_LN + E_LN1 + 2 * TILES, e_rs, w * 4 + 4)

            def fourth_apply(w, j):
                normal_tile(ox[:, 1, j, :], xres[:, 1, j, :], ln_e, KT + j).then_inc(e_ln, 1)

            def fourth_scale(w, j):
                scale_tile(ox[:, 0, j, :], xres[:, 0, j, :], ln_e, j, mod_b[:, 0, 2, :]).then_inc(e_ln, 1)

            def fourth_shift(w, j):
                if j == 0:
                    dve.wait_ge(e_ln, w * E_LN + E_LN1 + E_READY + KT)
                shift_tile(ox[:, 0, j, :], ox[:, 0, j, :], ln_e, j, mod_b[:, 0, 1, :]).then_inc(e_ln, 1)

            def h_lo(w, c):
                dve.wait_ge(hh_done, w * DC + c + 1)
                sub(ht_l[:, c, :], ht_bank(w, c), ht_h[:, c, :].bitcast(F32)).then_inc(hl_done, 1)

            def relu_lo(w, m):
                dve.wait_ge(rh_done, w * DC + m + 1)
                dve.scalar_tensor_tensor(rt_l[:, m, :], pair_bank(w, m), 0.0, rt_h[:, m, :].bitcast(F32),
                                         ALU.max, ALU.subtract).then_inc(rl_done, 1)

            def gate_top(w):
                dve.wait_ge(ex_done, w * TILES + TILES)
                dve.memset(g_w[:, :], 0.0)
                for j in range(TILES):
                    dve.max(top[:, j, :], ex[:, j, D:EG]).then_inc(gate, 1)
                dve.wait_ge(gate, w * GATE + 4)
                dve.tensor_tensor(g_d[:, :, :], top[:, :, 0:2], top[:, :, 0:1].to_broadcast([P, TILES, 2]),
                                  ALU.subtract).then_inc(gate, 1)

            def gate_weight(w):
                dve.wait_ge(gate_exp, w + 1)
                dve.tensor_tensor(g_s[:, :], g_e[:, :, 0], g_e[:, :, 1], ALU.add).then_inc(gate, 1)
                dve.wait_ge(gate, w * GATE + 6)
                dve.reciprocal(g_i[:, :], g_s[:, :]).then_inc(gate, 1)
                dve.wait_ge(gate, w * GATE + 7)
                dve.tensor_tensor(g_r[:, :, :], g_e[:, :, :], g_i[:, :].unsqueeze(2).to_broadcast([P, TILES, 2]),
                                  ALU.mult).then_inc(gate, 1)
                dve.wait_ge(gate, w * GATE + 8)
                dve.tensor_tensor(g_w[:, :], g_r[:, :, 0], g_r[:, :, 1], ALU.add).then_inc(gate, 1)

            def combine(w, b):
                dve.wait_ge(shared_done, w * 2 + b + 1)
                if b == 0:
                    dve.wait_ge(gate, w * GATE + GATE)
                for j in range(KT):
                    i = b * KT + j
                    dve.scalar_tensor_tensor(ox[:, b, j, :], ex[:, i, 0:D], g_w[:, i:i + 1],
                                             pair_bank(w, b)[:, j * D:(j + 1) * D],
                                             ALU.mult, ALU.add).then_inc(f_done, 1)

            def between(s, slot):
                t, at = s.t, (s.h, slot)
                if not s.first:
                    if at == (0, 3):
                        v_lo(t)
                    if at == (2, 0):
                        take_out(t - 1, s)
                    if at == (2, 3):
                        third_stats(t - 1, 0)
                        third_stats(t - 1, 1)
                        third_stats(t - 1, 2)
                    if at == (3, 1):
                        third_stats(t - 1, 3)
                    if at == (3, 3):
                        third_means(t - 1)
                    if at == (4, 0):
                        third_newton(t - 1)
                    if at == (4, 1):
                        third_apply(t - 1, 0)
                    if at == (4, 3):
                        third_apply(t - 1, 1)
                        third_scale(t - 1, 0)
                        third_scale(t - 1, 1)
                    if at == (5, 0):
                        third_shift(t - 1, 0)
                    if at == (5, 1):
                        third_shift(t - 1, 1)
                    if at == (5, 3):
                        fourth_stats(t - 1, 0)
                        fourth_stats(t - 1, 1)
                        fourth_stats(t - 1, 2)
                        fourth_stats(t - 1, 3)
                    if at == (6, 0):
                        fourth_means(t - 1)
                    if at == (6, 3):
                        fourth_newton(t - 1)
                    if at == (7, 0):
                        fourth_apply(t - 1, 0)
                        fourth_apply(t - 1, 1)
                    if at == (7, 3):
                        fourth_scale(t - 1, 0)
                        fourth_scale(t - 1, 1)
                    if at == (8, 0):
                        fourth_shift(t - 1, 0)
                    if at == (8, 1):
                        fourth_shift(t - 1, 1)
                    if at == (8, 3):
                        h_lo(t - 1, 0)
                    if at == (9, 1):
                        h_lo(t - 1, 1)
                    if at == (9, 3):
                        relu_lo(t - 1, 0)
                    if at == (10, 1):
                        relu_lo(t - 1, 1)
                    if at == (12, 1):
                        gate_top(t - 1)
                    if at == (13, 0):
                        gate_weight(t - 1)
                    if at == (13, 1):
                        combine(t - 1, 0)
                    if at == (13, 3):
                        combine(t - 1, 1)
                if not s.last:
                    if at == (1, 3):
                        first_stats(t + 1, 0)
                        first_stats(t + 1, 1)
                        first_stats(t + 1, 2)
                    if at == (2, 1):
                        first_stats(t + 1, 3)
                    if at == (3, 0):
                        first_means(t + 1)
                    if at == (3, 3):
                        first_newton(t + 1)
                    if at == (6, 0):
                        p_apply(t + 1, 0)
                    if at == (6, 1):
                        p_apply(t + 1, 1)
                    if at == (7, 1):
                        p_apply(t + 1, 2)
                    if at == (8, 3):
                        p_apply(t + 1, 3)
                    if at == (9, 0):
                        second_stats(t + 1, 0)
                    if at == (9, 3):
                        second_stats(t + 1, 1)
                    if at == (10, 0):
                        second_stats(t + 1, 2)
                    if at == (10, 3):
                        second_stats(t + 1, 3)
                        second_means(t + 1)
                    if at == (11, 0):
                        second_newton(t + 1)
                    if at == (11, 1):
                        p_apply(t + 1, 0)
                    if at == (11, 3):
                        p_apply(t + 1, 1)
                        p_apply(t + 1, 2)
                        p_apply(t + 1, 3)
                    if at == (12, 3):
                        xn_lo(t + 1, 0)
                    if at == (14, 1):
                        xn_lo(t + 1, 1)
                    if at == (15, 1):
                        k_norms(t + 1)
                    if at == (15, 3):
                        k_lo(t + 1)

            def step(s):
                if s.h == 0:
                    x_move(s)
                between(s, 0)
                if s.has(1):
                    sq_lo(s)
                between(s, 1)
                p_hi(s, 0)
                p_hi(s, 1)
                p_lo(s, 0)
                p_lo(s, 1)
                between(s, 2)
                if s.has(1):
                    q_norms(s)
                    q_lo(s)
                between(s, 3)
                if s.has(-1):
                    o_norm(s)

            def wq_lo(i):
                dve.wait_ge(w_hi, i + 1)
                sub(wq_l[:, i, :], late[:, i, :], wq_h[:, i, :].bitcast(F32)).then_inc(w_lo, 1)

            def wo_lo(i):
                dve.wait_ge(w_hi, i + 3)
                sub(wo_l[:, 8 * i:8 * (i + 1), :], late[:, i, :].rearrange("p (h n) -> p h n", n=D),
                    wo_h[:, 8 * i:8 * (i + 1), :].bitcast(F32)).then_inc(w_lo, 1)

            def rows(m):
                return m.unsqueeze(1).to_broadcast([P, KT, D])

            dve.memset(eps_ln[:, :], LN_EPS).then_inc(eps_done, 1)
            dve.memset(eps_q[:, :], L2_EPS / (SCALE * SCALE) * ONE).then_inc(eps_done, 1)
            dve.memset(eps_k[:, :], L2_EPS * ONE).then_inc(eps_done, 1)
            dve.memset(fones, ONE).then_inc(ones_done, 1)
            dve.wait_ge(ones_done, 1)
            dve.tensor_copy(ones[:, :], fones).then_inc(ones_done, 1)
            dve.wait_ge(c_exp, 1)
            dve.tensor_scalar(c_e[:, :, :], c_e[:, :, :], 1.0, None, ALU.add).then_inc(c_chain, 1)
            dve.wait_ge(c_chain, 1)
            dve.reciprocal(c_s[:, :, :], c_e[:, :, :]).then_inc(c_chain, 1)
            dve.wait_ge(c_chain, 2)
            dve.tensor_tensor(c_s[:, :, :], c_sb[:, :, :], c_s[:, :, :], ALU.mult).then_inc(c_chain, 1)
            for i in range(TILES):
                first_stats(0, i)
            first_means(0)
            first_newton(0)
            for i in range(TILES):
                p_apply(0, i)
            banks = (ps_sim[0:B, 0, :], ps_sim[0:B, 1, :], ps_o[0:B, :])
            fixed = 0

            def row(k):
                return mod_rows[k // 4][:, k % 4, :]

            def fix(ins):
                nonlocal fixed
                fixed += 1
                ins.then_inc(mod_fix, 1)

            dve.wait_ge(mod_mm, 1)
            fix(dve.tensor_copy(row(0), banks[0][:, 0:D]))
            fix(dve.tensor_scalar(row(1), banks[0][:, D:2 * D], 1.0, None, ALU.add))
            dve.wait_ge(wkv_hi, 1)
            sub(wkv_l[:, :, :], ss[:, :].rearrange("p (c n) -> p c n", c=DC), wkv_h[:, :, :].bitcast(F32)).then_inc(wkv_lo, 1)
            dve.wait_ge(mod_mm, 3)
            dve.wait_ge(gout_in, 16)
            dve.wait_ge(wkv_lo, 1)
            gates = ((2, banks[1][:, 0:D], ss[0:B, 0:D]), (5, banks[2][:, D:2 * D], ss[0:B, D:2 * D]))
            for k, g, two in gates:
                fix(dve.tensor_scalar(two, g, 0.0, 2.0, ALU.is_ge, ALU.mult))
            fix(dve.tensor_copy(row(3), banks[1][:, D:2 * D]))
            dve.wait_ge(mod_fix, fixed - 1)
            for k, g, two in gates:
                fix(dve.scalar_tensor_tensor(row(k), two, -1.0, g, ALU.add, ALU.mult))
            fix(dve.tensor_scalar(row(4), banks[2][:, 0:D], 1.0, None, ALU.add))
            dve.wait_ge(mod_fix, fixed - 1)
            for k, g, two in gates:
                fix(dve.tensor_scalar(row(k), row(k), 0.25, None, ALU.max))
            dve.wait_ge(mod_fix, fixed)
            for k, g, two in gates:
                fix(dve.scalar_tensor_tensor(row(k), two, -1.0, row(k), ALU.add, ALU.mult))
            dve.wait_ge(mod_fix, fixed)
            fix(dve.tensor_tensor(row(2), row(2), gout16, ALU.mult))
            assert fixed == MOD_FIX
            dve.wait_ge(moda_in, 16)
            dve.wait_ge(p_ln, P_LN1)
            for k, op in ((1, ALU.mult), (0, ALU.add)):
                dve.tensor_tensor(xin[:, 0, :, :], xin[:, 0, :, :], rows(mod_a[:, 0, k, :]), op).then_inc(start_mod, 1)
                dve.wait_ge(start_mod, 2 - k)
            for i in range(TILES):
                second_stats(0, i)
            second_means(0)
            second_newton(0)
            for i in range(TILES):
                p_apply(0, i)
            wq_lo(0)
            dve.wait_ge(gn_in, 16)
            xn_lo(0, 0)
            xn_lo(0, 1)
            wq_lo(1)
            k_norms(0)
            sq_lo(START[1])
            k_lo(0)
            v_lo(0)
            wo_lo(0)
            q_norms(START[1])
            q_lo(START[1])
            wo_lo(1)
            run(dve, step)
            o_norm(END[0])
            w = PAIRS - 1
            take_out(w, END[1])
            for i in range(TILES):
                third_stats(w, i)
            third_means(w)
            third_newton(w)
            third_apply(w, 0)
            third_apply(w, 1)
            third_scale(w, 0)
            third_scale(w, 1)
            third_shift(w, 0)
            third_shift(w, 1)
            for i in range(TILES):
                fourth_stats(w, i)
            fourth_means(w)
            fourth_newton(w)
            fourth_apply(w, 0)
            fourth_apply(w, 1)
            fourth_scale(w, 0)
            fourth_scale(w, 1)
            fourth_shift(w, 0)
            fourth_shift(w, 1)
            for c in range(DC):
                h_lo(w, c)
            for m_ in range(DC):
                relu_lo(w, m_)
            gate_top(w)
            gate_weight(w)
            combine(w, 0)
            combine(w, 1)
            dve.wait_ge(f_done, w * TILES + TILES)
            dve.tensor_tensor(ox[:, 1, :, :], ox[:, 1, :, :], rows(mod_b[:, 1, 3, :]), ALU.mult).then_inc(tail_done, 1)
            dve.wait_ge(tail_done, 1)
            dve.tensor_tensor(ox[:, 1, :, :], ox[:, 1, :, :], xres[:, 1, :, :], ALU.add).then_inc(tail_done, 1)

        @block.gpsimd
        def _(pool):
            def tt(o, a, b, op):
                return pool.tensor_tensor(o, a, b, op)

            def rows(m):
                return m.unsqueeze(1).to_broadcast([P, KT, D])

            def p_sum(s):
                pool.wait_ge(exp_done, s.n(0, KT))
                after(pool, ssl_done, s.n(-1))
                tt(ss[:, :], pr[:, 0, :], pr[:, 1, :], ALU.add).then_inc(ss_done, 1)

            def ss_lo(s):
                pool.wait_ge(ssh_done, s.n(0))
                tt(ss_l[:, :], ss[:, :], ss_h[:, :].bitcast(F32), ALU.subtract).then_inc(ssl_done, 1)

            def o_lo(s):
                pool.wait_ge(oh_done, s.n(-2))
                tt(o_l[:, :], on, o_h[:, :].bitcast(F32), ALU.subtract).then_inc(ol_done, 1)

            def modulate_in(u, b, k):
                if k == 0:
                    pool.wait_ge(p_ln, u * P_LN + (P_LN1 - TILES + (b + 1) * KT))
                    pool.wait_ge(moda_in, u * 16 + 16)
                    tt(xin[:, b, :, :], xin[:, b, :, :], rows(mod_a[:, b, 1, :]), ALU.mult).then_inc(p_mod, 1)
                else:
                    pool.wait_ge(p_mod, u * P_MOD + (2 * b + 1))
                    tt(xin[:, b, :, :], xin[:, b, :, :], rows(mod_a[:, b, 0, :]), ALU.add).then_inc(p_mod, 1)

            def ksq_lo(u):
                pool.wait_ge(ksqh_done, u + 1)
                tt(ksq_l[:, :], ksq, ksq_h[:, :].bitcast(F32), ALU.subtract).then_inc(ksql_done, 1)

            def residual(w, k):
                if k == 0:
                    pool.wait_ge(e_ln, w * E_LN + E_READY)
                    pool.wait_ge(modb_in, w * 16 + 16)
                    pool.wait_ge(xres_in, w * 16 + 16)
                    tt(ox[:, 1, :, :], ox[:, 1, :, :], rows(mod_b[:, 1, 0, :]), ALU.mult).then_inc(e_mod, 1)
                else:
                    pool.wait_ge(e_mod, w * E_MOD + 1)
                    tt(xres[:, 1, :, :], xres[:, 1, :, :], ox[:, 1, :, :], ALU.add).then_inc(e_mod, 1)

            def modulate_mlp(w, k):
                if k == 0:
                    pool.wait_ge(e_ln, w * E_LN + E_LN1 + E_READY)
                    tt(ox[:, 1, :, :], ox[:, 1, :, :], rows(mod_b[:, 1, 2, :]), ALU.mult).then_inc(e_mod, 1)
                else:
                    pool.wait_ge(e_mod, w * E_MOD + 3)
                    tt(ox[:, 1, :, :], ox[:, 1, :, :], rows(mod_b[:, 1, 1, :]), ALU.add).then_inc(e_mod, 1)

            def finish(w, b, k):
                if k == 0:
                    pool.wait_ge(f_done, w * TILES + (b + 1) * KT)
                    tt(ox[:, b, :, :], ox[:, b, :, :], rows(mod_b[:, b, 3, :]), ALU.mult).then_inc(e_mod, 1)
                else:
                    pool.wait_ge(e_mod, w * E_MOD + (4 + 2 * b + 1))
                    tt(ox[:, b, :, :], ox[:, b, :, :], xres[:, b, :, :], ALU.add).then_inc(e_mod, 1)

            def between(s, k):
                h, t = s.h, s.t
                if not s.last:
                    if h == 6:
                        modulate_in(t + 1, 0, k)
                    if h == 8 and k == 1:
                        modulate_in(t + 1, 1, 0)
                    if h == 9 and k == 0:
                        modulate_in(t + 1, 1, 1)
                    if h == 14 and k == 0:
                        ksq_lo(t + 1)
                if not s.first:
                    if h == 4 and k == 1:
                        residual(t - 1, 0)
                    if h == 5 and k == 0:
                        residual(t - 1, 1)
                    if h == 7:
                        modulate_mlp(t - 1, k)
                    if h == 13:
                        finish(t - 1, 0, k)
                    if h == 15:
                        finish(t - 1, 1, k)

            def step(s):
                if s.has(-2):
                    o_lo(s)
                p_sum(s)
                between(s, 0)
                ss_lo(s)
                between(s, 1)

            pool.memset(ident[:, :], 0.0).then_inc(const_zero, 1)
            pool.wait_ge(const_zero, 1)
            pool.affine_select(out=ident[:, :], in_=ident[:, :], compare_op=ALU.not_equal, fill=1.0, base=0,
                               pattern=[[-1, P]], channel_multiplier=1).then_inc(const_done, 1)
            pool.wait_ge(mod_fix, 2)
            pool.dma_start(scratch[:, 0:2, :], mod_rows[0][:, 0:2, :]).then_inc(moda_stored, 16)
            def split2(i):
                stage2 = ex[:, :, :].rearrange("p j n -> p (j n)")
                hi, lo, n = ((weg_h, weg_l, EG), (wup_h, wup_l, D), (wdn_h, wdn_l, D))[i]
                src = stage2[:, 0:DC * n].rearrange("p (c n) -> p c n", c=DC)
                pool.wait_ge(w2_in, 32 + 16 * i)
                pool.tensor_copy(hi[:, :, :], src).then_inc(w2_hi, 1)
                pool.wait_ge(w2_hi, i + 1)
                tt(lo[:, :, :], src, hi[:, :, :].bitcast(F32), ALU.subtract).then_inc(w2_lo, 1)

            split2(0)
            pool.wait_ge(mod_fix, MOD_FIX)
            pool.dma_start(scratch[:, 2:4, :], mod_rows[0][:, 2:4, :]).then_inc(modb_stored, 16)
            pool.dma_start(scratch[:, 4:6, :], mod_rows[1]).then_inc(modb_stored, 16)
            pool.wait_ge(p_ln, P_LN1)
            pool.wait_ge(moda_in, 16)
            for k, op in ((1, ALU.mult), (0, ALU.add)):
                tt(xin[:, 1, :, :], xin[:, 1, :, :], rows(mod_a[:, 1, k, :]), op).then_inc(p_mod, 2)
                pool.wait_ge(p_mod, 2 * (2 - k))
            split2(1)
            ksq_lo(0)
            split2(2)
            run(pool, step)
            o_lo(END[0])
            o_lo(END[1])
            w = PAIRS - 1
            for k in range(2):
                residual(w, k)
            for k in range(2):
                modulate_mlp(w, k)
            for k in range(2):
                finish(w, 0, k)


def kernel(L0_attn_x, L0_attn_g_norm, L0_attn_Wq, L0_attn_Wkv, L0_attn_Wout, L0_attn_g_out, L0_ffn_W_up,
           L0_ffn_W_down, L0_ffn_W_gate, L0_ffn_W_expert, L0_c, L0_wmod):
    import numpy as np
    import concourse.bacc as bacc
    from concourse.bass_utils import run_bass_kernel_spmd

    nc = bacc.Bacc("TRN2", target_bir_lowering=False, num_devices=1)
    arrays = {
        "x": L0_attn_x, "g_norm_pc": np.transpose(np.reshape(L0_attn_g_norm, (DC, P))), "wq": L0_attn_Wq, "wkv": L0_attn_Wkv, "wo": L0_attn_Wout,
        "g_out": L0_attn_g_out, "wup_t": np.transpose(L0_ffn_W_up), "wdown_t": np.transpose(L0_ffn_W_down),
        "wgate_t": np.transpose(L0_ffn_W_gate), "wexp": L0_ffn_W_expert, "c_t": np.transpose(L0_c), "wmod": L0_wmod,
    }
    arrays = {name: np.ascontiguousarray(a) for name, a in arrays.items()}
    args = [nc.dram_tensor(name, a.shape, mybir.dt.from_np(a.dtype), kind="ExternalInput").ap()
            for name, a in arrays.items()]
    scratch = nc.dram_tensor("modulation", (B, 6, D), F32, kind="Internal").ap()
    out = nc.dram_tensor("out", (B, N, D), F32, kind="ExternalOutput").ap()
    adaln_block(nc, *args, scratch, out)
    r = run_bass_kernel_spmd(nc, [arrays], core_ids=[0])
    return r.results[0]["out"]
```
